# Optimizing a Trainium2 kernel written in Bass

```python
import numpy as np
import jax
import jax.numpy as jnp

def _softmax(x, axis=-1):
    return jax.nn.softmax(x, axis=axis)

def _gelu(x):
    return jax.nn.gelu(x, approximate=True)

def _silu(x):
    return jax.nn.silu(x)

def _sigmoid(x):
    return jax.nn.sigmoid(x)

def _layernorm(x, axis=-1, eps=1e-05):
    m = jnp.mean(x, axis=axis, keepdims=True)
    v = jnp.var(x, axis=axis, keepdims=True)
    return (x - m) / jnp.sqrt(v + eps)

def _scatter_add(tgt, idx, src, axis=0):
    return tgt.at[idx].add(src)

def _segment_sum(src, seg, n):
    return jax.ops.segment_sum(src, seg, n)
kernel_name = 'mk_gnn_ffn_d1_gnn_r64_bcdd99'

def setup_inputs(seed: int=0):
    np.random.seed(seed)
    _w = jnp.asarray

    def _rec_inputs():
        import jax
        import jax.numpy as jnp
        _gk = jax.random.key(seed)
        x = -6.415e-05 + 1 * jax.random.normal(jax.random.fold_in(_gk, 1), (10000, 512), jnp.float32)
        src = jax.random.randint(jax.random.fold_in(_gk, 2), (2500,), 0, 10000, jnp.int32)
        dst = jnp.minimum((10000 * jax.random.uniform(jax.random.fold_in(_gk, 3), (2500,)) ** 2.0).astype(jnp.int32), 9999)
        _o = jnp.argsort(dst, stable=True)
        src = src[_o]
        dst = dst[_o]
        edge_attr_512 = -8.16379e-05 + 0.999858 * jax.random.normal(jax.random.fold_in(_gk, 12), (2500, 512), jnp.float32)
        return (x, src, dst, edge_attr_512)
    x, src, dst, edge_attr_512 = _rec_inputs()

    def _L0_gnn_setup():
        import jax, jax.numpy as jnp
        import numpy as np
        N_NODES = 20000
        N_EDGES = 3125
        N_SEG = 16
        EXTENT = 32
        N_PATHS = 64
        OP_SIZE = N_SEG * EXTENT
        key = jax.random.key(seed)
        k1, k2, k3, k4, k5, k6 = jax.random.split(key, 6)
        x_nodes = jax.random.normal(k1, (N_NODES, OP_SIZE), dtype=jnp.float32)
        x_edges = jax.random.normal(k2, (N_EDGES, OP_SIZE), dtype=jnp.float32)
        path_coeffs = jax.random.normal(k3, (N_PATHS,), dtype=jnp.float32)
        src = jax.random.randint(k4, (N_EDGES,), 0, N_NODES, dtype=jnp.int64)
        dst = jax.random.randint(k5, (N_EDGES,), 0, N_NODES, dtype=jnp.int64)
        path_indices = jax.random.randint(k6, (N_PATHS, 3), 0, N_SEG, dtype=jnp.int64)
        return {'x_nodes': x_nodes, 'x_edges': x_edges, 'path_coeffs': path_coeffs, 'src': src, 'dst': dst, 'path_indices': path_indices}
    _L0_gnn_all = _L0_gnn_setup()
    _L0_gnn_in = {k: v for k, v in _L0_gnn_all.items() if k in ('path_coeffs', 'path_indices')}
    del _L0_gnn_all

    def _L0_ffn_setup():
        import jax, jax.numpy as jnp
        import numpy as np
        K = 2
        key = jax.random.key(seed)
        ks = jax.random.split(key, 6)
        B, T, d, E, dff = (2, 32, 512, 8, 32)
        x = jax.random.normal(ks[0], (B, T, d), dtype=jnp.float32)
        Wg = jax.random.normal(ks[1], (d, E), dtype=jnp.float32) * 0.02
        W1 = jax.random.normal(ks[2], (E, d, dff), dtype=jnp.float32) * 0.02
        b1 = jnp.zeros((E, dff), dtype=jnp.float32)
        W2 = jax.random.normal(ks[3], (E, dff, d), dtype=jnp.float32) * 0.02
        b2 = jnp.zeros((E, d), dtype=jnp.float32)
        return {'x': x, 'Wg': Wg, 'W1': W1, 'b1': b1, 'W2': W2, 'b2': b2}
    _L0_ffn_all = _L0_ffn_setup()
    _L0_ffn_in = {k: v for k, v in _L0_ffn_all.items() if k in ('Wg', 'W1', 'b1', 'W2', 'b2')}
    del _L0_ffn_all
    return {'x': x, 'src': src, 'dst': dst, 'edge_attr_512': edge_attr_512, 'L0_gnn_path_coeffs': _L0_gnn_in['path_coeffs'], 'L0_gnn_path_indices': _L0_gnn_in['path_indices'], 'L0_ffn_Wg': _L0_ffn_in['Wg'], 'L0_ffn_W1': _L0_ffn_in['W1'], 'L0_ffn_b1': _L0_ffn_in['b1'], 'L0_ffn_W2': _L0_ffn_in['W2'], 'L0_ffn_b2': _L0_ffn_in['b2']}

def reference(x, src, dst, edge_attr_512, L0_gnn_path_coeffs, L0_gnn_path_indices, L0_ffn_Wg, L0_ffn_W1, L0_ffn_b1, L0_ffn_W2, L0_ffn_b2):
    import jax
    import jax.numpy as jnp

    def _L0_gnn_ref(x_nodes, x_edges, path_coeffs, src, dst, path_indices):
        import jax, jax.numpy as jnp
        import numpy as np
        N_NODES = 20000
        N_EDGES = 3125
        N_SEG = 16
        EXTENT = 32
        N_PATHS = 64
        OP_SIZE = N_SEG * EXTENT
        n_nodes = x_nodes.shape[0]
        x1 = x_nodes[src].reshape(-1, N_SEG, EXTENT)
        x2 = x_edges.reshape(-1, N_SEG, EXTENT)
        i1, i2, i3 = (path_indices[:, 0], path_indices[:, 1], path_indices[:, 2])
        contrib = path_coeffs[None, :, None] * x1[:, i1, :] * x2[:, i2, :]
        edge_out = jnp.zeros((x2.shape[0], N_SEG, EXTENT), x_nodes.dtype).at[:, i3, :].add(contrib)
        out = jnp.zeros((n_nodes, OP_SIZE), x_nodes.dtype).at[dst].add(edge_out.reshape(-1, OP_SIZE))
        return out

    def _L0_ffn_ref(x, Wg, W1, b1, W2, b2):
        import jax, jax.numpy as jnp
        import numpy as np
        K = 2
        logits = jnp.einsum('btd,de->bte', x, Wg)
        probs = jax.nn.softmax(logits, axis=-1)
        top_p, _top_i = jax.lax.top_k(probs, K)
        top_p = top_p / jnp.sum(top_p, axis=-1, keepdims=True)
        b2_sum = jnp.sum(b2, axis=0)
        out = jnp.zeros_like(x)
        for i in range(K):
            w_in = x * top_p[..., i:i + 1]
            h = jax.nn.gelu(jnp.einsum('btd,edf->ebtf', w_in, W1) + b1[:, None, None, :], approximate=False)
            out = out + jnp.einsum('ebtf,efd->btd', h, W2) + b2_sum
        return out
    x = x + _L0_gnn_ref(_layernorm(x, axis=-1), edge_attr_512, L0_gnn_path_coeffs, src, dst, L0_gnn_path_indices)
    x = x + _L0_ffn_ref(_layernorm(x, axis=-1)[None], L0_ffn_Wg, L0_ffn_W1, L0_ffn_b1, L0_ffn_W2, L0_ffn_b2)[0]
    return x

_drawn_inputs = setup_inputs


def setup_inputs(seed=0):
    import zlib

    import numpy as np

    out = dict(_drawn_inputs(seed))
    spreads = {'L0_ffn_b1': (0.0, 0.35), 'L0_ffn_b2': (0.0, 0.1)}
    factors = {'L0_ffn_Wg': 8.0}
    for name, (base, spread) in spreads.items():
        noise = np.random.default_rng([zlib.crc32(name.encode()), seed]).standard_normal(out[name].shape)
        drawn = base * np.exp(spread * noise) if base else spread * noise
        out[name] = jnp.asarray(drawn.astype(out[name].dtype))
    for name, factor in factors.items():
        out[name] = (out[name] * factor).astype(out[name].dtype)
    return out
```

```python
import numpy as np
import concourse.bass as bass
from concourse import mybir
from contextlib import ExitStack


def gnn_ffn_kernel(nc, x, src, dst, edge_attr, path_coeffs, path_indices, Wg, W1, b1, W2, b2, out):
    F32 = mybir.dt.float32
    F32R = mybir.dt.float32r
    BF16 = mybir.dt.bfloat16
    I32 = mybir.dt.int32
    ALU = mybir.AluOpType
    ACT = mybir.ActivationFunctionType

    N, D = x.shape
    NE = src.shape[0]
    NP = path_coeffs.shape[0]
    EXPERTS, _, DFF = W1.shape
    HID = EXPERTS * DFF
    WC = HID + EXPERTS
    EXTENT = 32
    NSEG = D // EXTENT
    EPS = 1e-5
    P = 128
    DC = D // P
    HC = HID // P

    ET = 20
    EP = NE // ET
    assert EP * ET == NE and EP <= P
    SET = ET // 2
    SETS = 2

    RING = 12
    PAIRS = RING // 2
    ORING = 4
    FIRST = 4
    MAIN_PAIRS = -(-N // (2 * P))
    MAIN = 2 * MAIN_PAIRS
    TILES = MAIN + ET
    ROUNDS = (TILES - FIRST) // RING
    assert FIRST + ROUNDS * RING == TILES and MAIN % ORING == 0
    L_SCALE, L_HT, L_DOWN, L_FINAL, L_STORE, L_GATHER = 2, 4, 5, 6, 7, 5
    SET0, SET1, SUM1 = (1, 3), (3, 5), 5
    PPR = NP // 2
    PER_SLOT = [3] * 10 + [2, 0]
    PB = 4
    SRC_PER = 4
    SRC_SLOTS = RING - ET // SRC_PER - 1
    FILLS_LOOPED = 10
    FILLS = RING + FILLS_LOOPED * (SET0[1] - SET0[0])
    FILL = N * D // FILLS
    assert FILL * FILLS == N * D and FILL % 16 == 0
    assert sum(PER_SLOT) == PPR and len(PER_SLOT) == RING

    y_rows = nc.dram_tensor("y_rows", (N + P, D), F32, kind="Internal").ap()
    y_flat = y_rows.rearrange("n d -> (n d)")
    x_flat = x.rearrange("n d -> (n d)")

    def pair_rows(dram, q):
        base = q * 2 * P
        if isinstance(q, int):
            base = min(base, N - 2 * P)
        return dram[bass.ds(base, 2 * P), :].rearrange("(p j) d -> p j d", j=2)

    ctx = ExitStack()
    with ctx:
        def sb(name, shape, dt=F32):
            return ctx.enter_context(nc.sbuf_tensor(name, shape, dt))

        def pb(name, shape):
            return ctx.enter_context(nc.psum_tensor(name, shape, F32))

        def sem(name):
            return ctx.enter_context(nc.semaphore(name))

        rows = sb("rows", [P, RING, D])
        outs = sb("outs", [P, ORING, D])
        x1 = sb("x1", [P, ET, D])
        x2 = sb("x2", [P, ET, D])
        acc = sb("acc", [P, ET, D])
        same = sb("same", [P, ET, EP], BF16)
        same_now = sb("same_now", [P, EP])
        prod = [sb(f"prod{i}", [P, SET, EXTENT]) for i in range(PB)]
        yT_hi = [sb(f"yT_hi{i}", [P, D], F32R) for i in range(2)]
        yT_lo = [sb(f"yT_lo{i}", [P, D], F32R) for i in range(2)]
        w_hi = sb("w_hi", [P, DC, WC], F32R)
        w_lo = sb("w_lo", [P, DC, WC], F32R)
        w2_hi = sb("w2_hi", [P, HC, D], F32R)
        w2_lo = sb("w2_lo", [P, HC, D], F32R)
        hid = [sb(f"hid{i}", [P, 2, HID]) for i in range(2)]
        hsum = [sb(f"hsum{i}", [P, HID]) for i in range(2)]
        hT_hi = [sb(f"hT_hi{i}", [P, HID], F32R) for i in range(2)]
        hT_lo = [sb(f"hT_lo{i}", [P, HID], F32R) for i in range(2)]
        moved = [sb(f"moved{i}", [P, D]) for i in range(2)]
        b1_bc = sb("b1_bc", [P, HID])
        bias_rows = sb("bias_rows", [P, D], F32R)
        ones = sb("ones", [P, P], F32R)
        ident = sb("ident", [P, P])
        coef = sb("coef", [P, NP])
        table = sb("table", [1, NP * 3], I32)
        src_i = sb("src_i", [P, ET], I32)
        dst_i = sb("dst_i", [P, ET], I32)
        dst_f = sb("dst_f", [P, ET])
        repeats = sb("repeats", [P, ET])
        away = sb("away", [P, ET])
        lead_i = sb("lead_i", [P, ET], I32)
        spare_i = sb("spare_i", [P, 1], I32)
        spare_f = sb("spare_f", [P, 1])
        put_i = sb("put_i", [P, SET // 2], I32)
        src_stats = sb("src_stats", [P, ET, 6])
        src_mv = sb("src_mv", [P, ET, 2])
        src_rstd = sb("src_rstd", [P, ET])
        src_shift = sb("src_shift", [P, ET])
        stats = sb("stats", [P, 4, 6])
        mean_var = sb("mean_var", [P, 4, 2])
        var4 = sb("var4", [P, 4])
        half_rstd = sb("half_rstd", [P, 4])
        minus_half = sb("minus_half", [P, ET])
        top8 = sb("top8", [P, 4, 8])
        gap = sb("gap", [P, 4])
        half_gap = sb("half_gap", [P, 4])
        th = sb("th", [P, 4])
        scale = sb("scale", [P, 4, 2])

        yT = pb("yT", [P, D])
        U = [pb(f"U{i}", [P, 512]) for i in range(4)]
        HT = pb("HT", [P, 512])
        O = pb("O", [P, D])
        C = pb("C", [P, D])

        w_raw = outs[:, :, :].rearrange("p a d -> p (a d)")[:, 0:DC * WC].rearrange("p (c n) -> p c n", c=DC)
        w2_raw = [hid[h][:, :, :].rearrange("p a f -> p (a f)") for h in range(HC)]
        b2_raw = moved[0][0:EXPERTS, :]
        bias_lo = moved[1][0:1, :].bitcast(F32R)
        mean_mat = prod[0][:, :, :].rearrange("p t u -> p (t u)")[:, 0:P]
        twos = prod[1][:, :, :].rearrange("p t u -> p (t u)")[:, 0:P]
        all_dst = acc[:, :, :].rearrange("p t d -> p (t d)")[:, 0:NE].bitcast(I32) \
            .rearrange("p (e t) -> p e t", t=ET)
        dst_tiles = -(-NE // D)
        later = prod[3][:, :, :].rearrange("p t u -> p (t u)")[:, 0:P]
        scratch = prod[2][:, :, :].rearrange("p t u -> p (t u)")[0:EP, 0:EP]

        x_loaded = [sem(f"x_loaded{i}") for i in range(PAIRS)]
        edge_loaded = [sem(f"edge_loaded{i}") for i in range(RING)]
        w_loaded = sem("w_loaded")
        w2_loaded = sem("w2_loaded")
        bias_loaded = sem("bias_loaded")
        index_loaded = sem("index_loaded")
        all_dst_loaded = sem("all_dst_loaded")
        table_loaded = sem("table_loaded")
        attr_loaded = sem("attr_loaded")
        x1_loaded = [sem(f"x1_loaded{i}") for i in range(SETS)]
        pool_const = sem("pool_const")
        const_ready = sem("const_ready")
        col_mean = sem("col_mean")
        w_centered = sem("w_centered")
        w_rounded = sem("w_rounded")
        w_ready = sem("w_ready")
        bias_sum = sem("bias_sum")
        bias_hi_made = sem("bias_hi_made")
        bias_moved = sem("bias_moved")
        bias_zero = sem("bias_zero")
        src_stats_made = sem("src_stats_made")
        src_var_ready = sem("src_var_ready")
        src_rstd_step = sem("src_rstd_step")
        src_rstd_ready = sem("src_rstd_ready")
        src_shift_ready = sem("src_shift_ready")
        x1_ready = sem("x1_ready")
        dst_made = sem("dst_made")
        eq_made = sem("eq_made")
        lead_step = sem("lead_step")
        lead_ready = sem("lead_ready")
        scaled = sem("scaled")
        multiplied = sem("multiplied")
        prod_free = sem("prod_free")
        index_copied = sem("index_copied")
        y_filled = sem("y_filled")
        same_ready = sem("same_ready")
        comb_ready = sem("comb_ready")
        C_free = sem("C_free")
        summed = sem("summed")
        yT_ready = sem("yT_ready")
        yT_hi_ready = sem("yT_hi_ready")
        yT_lo_ready = sem("yT_lo_ready")
        U_ready = sem("U_ready")
        stats_made = sem("stats_made")
        var_ready = sem("var_ready")
        var4_made = sem("var4_made")
        rstd_ready = sem("rstd_ready")
        top_made = sem("top_made")
        gap_made = sem("gap_made")
        half_gap_ready = sem("half_gap_ready")
        tanh_ready = sem("tanh_ready")
        scale_ready = sem("scale_ready")
        hid_in_ready = sem("hid_in_ready")
        hid_ready = sem("hid_ready")
        hsum_ready = sem("hsum_ready")
        HT_ready = sem("HT_ready")
        hT_hi_ready = sem("hT_hi_ready")
        hT_lo_ready = sem("hT_lo_ready")
        O_ready = sem("O_ready")
        final_ready = sem("final_ready")
        stored = [sem(f"stored{i}") for i in range(ORING // 2)]
        scattered = sem("scattered")

        block = ctx.enter_context(nc.Block())

        def rounds(eng, slot):
            for k in range(-1, FIRST):
                slot(0, k, None)
            for k in range(FIRST, FIRST + RING):
                slot(0, k, None)
            for part, (r0, r1) in (("set0", SET0), ("set1", SET1)):
                with eng.Fori(r0, r1) as r:
                    for k in range(FIRST, FIRST + RING):
                        slot(r, k, part)
            for r in range(SUM1, ROUNDS):
                for k in range(FIRST, FIRST + RING):
                    slot(r, k, "sum1" if r == SUM1 else None)
            for k in range(FIRST, FIRST + L_STORE + 1):
                slot(ROUNDS, k, None)

        def live(r, k):
            return 0 <= r * RING + k < TILES if isinstance(r, int) else True

        def tile(r, k):
            return r * RING + k

        def is_edge(r, k):
            return isinstance(r, int) and r * RING + k >= MAIN

        def wait_rows(eng, r, k):
            if is_edge(r, k):
                eng.wait_ge(edge_loaded[k % RING], 16 * ((r * RING + k - MAIN) // RING + 1))
            else:
                eng.wait_ge(x_loaded[k % RING // 2], (r + k // RING) * 16 + 16)

        def slot_paths(k):
            first = sum(PER_SLOT[:k - FIRST])
            return range(first, first + PER_SLOT[k - FIRST])

        def set_tiles(part):
            return slice(0, SET) if part == "set0" else slice(SET, ET)

        def path_numbers(r, k, part):
            first = (r - (SET0 if part == "set0" else SET1)[0]) * PPR
            return [(j, first + j, (r - SET0[0]) * PPR + j) for j in slot_paths(k)]

        def load_segment(eng, path, column):
            return eng.value_load(table[0:1, bass.ds(path * 3 + column, 1)], min_val=0, max_val=NSEG - 1) * EXTENT

        def sum_tile(r, k, part):
            s = k - FIRST
            if part == "set1" and s % 2 == 0 and s // 2 < SET // 2:
                return (r - SET1[0]) * (SET // 2) + s // 2, s // 2 % 2
            if part == "sum1" and s < SET:
                return SET + s, s % 2
            return None, None

        @block.sync
        def _(sp):
            def load(q, i):
                sp.dma_start(rows[:, 2 * i:2 * i + 2, :], pair_rows(x, q)).then_inc(x_loaded[i], 16)

            def store(q, i):
                sp.dma_start(pair_rows(out, q), outs[:, 2 * (i % 2):2 * (i % 2) + 2, :]) \
                    .then_inc(stored[i % 2], 16)

            load(0, 0)
            for c in range(DC):
                sp.dma_start(w_raw[:, c, 0:HID].rearrange("p (e f) -> p e f", e=EXPERTS),
                             W1[:, c * P:(c + 1) * P, :].rearrange("e p f -> p e f")).then_inc(w_loaded, 16)
            sp.dma_start(w_raw[:, :, HID:WC], Wg.rearrange("(c p) e -> p c e", p=P)).then_inc(w_loaded, 16)
            for q in range(1, PAIRS):
                load(q, q)
            loops = (MAIN_PAIRS - PAIRS) // PAIRS
            with sp.Fori(0, loops) as r:
                for i in range(PAIRS):
                    q = r * PAIRS + i
                    sp.wait_ge(final_ready, q * 2 + 2)
                    store(q, i)
                    load(q + PAIRS, i)
            for q in range(loops * PAIRS, MAIN_PAIRS):
                sp.wait_ge(final_ready, 2 * q + 2)
                if q == MAIN_PAIRS - 1:
                    sp.wait_ge(stored[(q - 1) % 2], 16 * ((q - 1) // 2 + 1))
                store(q, q % PAIRS)
                if q + PAIRS < MAIN_PAIRS:
                    load(q + PAIRS, q % PAIRS)
            for i in range(2):
                sp.wait_ge(stored[i], 16 * (MAIN_PAIRS // 2))

        @block.scalar
        def _(act):
            act.dma_start(src_i[0:EP, :], src.rearrange("(p t) -> p t", t=ET)).then_inc(index_loaded, 16)
            act.dma_start(dst_i[0:EP, :], dst.rearrange("(p t) -> p t", t=ET)).then_inc(index_loaded, 16)
            act.dma_start(b2_raw, b2).then_inc(bias_loaded, 16)
            act.dma_start(b1_bc[:, :], b1.rearrange("e f -> (e f)").partition_broadcast(P)).then_inc(bias_loaded, 16)
            for h in range(HC):
                act.dma_start(w2_raw[h], W2.rearrange("e f d -> (e f) d")[h * P:(h + 1) * P, :]) \
                    .then_inc(w2_loaded, 16)
            act.dma_start(all_dst[0:EP, :, :], dst.rearrange("(p t) -> p t", t=ET).partition_broadcast(EP)) \
                .then_inc(all_dst_loaded, 16)
            act.dma_start(table[0:1, :], path_indices.rearrange("n c -> (n c)").unsqueeze(0)) \
                .then_inc(table_loaded, 16)
            act.dma_start(coef[:, :], path_coeffs.partition_broadcast(P)).then_inc(table_loaded, 16)
            attr = edge_attr.rearrange("(p t) d -> p (t d)", t=ET)
            even = EP // 8 * 8
            for lo, hi in ((0, even), (even, EP)):
                act.dma_start(x2[lo:hi, :, :].rearrange("p t d -> p (t d)"), attr[lo:hi, :]) \
                    .then_inc(attr_loaded, 16)

            act.wait_ge(w_centered, 1)
            nc.scalar.activation(w_hi[:, :, :], w_raw, ACT.Copy).then_inc(w_rounded, 1)
            act.wait_ge(w2_loaded, 16 * HC)
            for h in range(HC):
                last = nc.scalar.activation(w2_hi[:, h, :], w2_raw[h], ACT.Copy)
            last.then_inc(w_rounded, 1)
            act.wait_ge(bias_sum, 1)
            act.wait_ge(bias_zero, 1)
            nc.scalar.activation(bias_rows[0:1, :], C[0:1, :], ACT.Copy).then_inc(bias_hi_made, 1)
            act.wait_ge(C_free, 1)
            act.dma_start(bias_rows[1:2, :].bitcast(F32), bias_lo.bitcast(F32)).then_inc(bias_moved, 16)

            def slot(r, k, part):
                s = k - FIRST
                if part == "set0" and s < FILLS_LOOPED or isinstance(r, int) and r == 0 and 0 <= s < RING:
                    f = s if part is None else RING + (r - SET0[0]) * FILLS_LOOPED + s
                    act.dma_start(y_flat[bass.ds(f * FILL, FILL)].rearrange("(a r) -> a r", a=16),
                                  x_flat[bass.ds(f * FILL, FILL)].rearrange("(a r) -> a r", a=16)) \
                        .then_inc(y_filled, 16)
                if live(r, k + 1):
                    act.wait_ge(yT_ready, tile(r, k + 2))
                    if live(r, k - 1):
                        act.wait_ge(U_ready, tile(r, k))
                    nc.scalar.activation(yT_hi[(k + 1) % 2][:, :], yT[:, :], ACT.Copy).then_inc(yT_hi_ready, 1)
                if k % 2 == 0 and live(r, k - L_SCALE):
                    act.wait_ge(half_gap_ready, r * PAIRS + k // 2)
                    c = (k - L_SCALE) % 4
                    nc.scalar.activation(th[:, c:c + 2], half_gap[:, c:c + 2], ACT.Tanh).then_inc(tanh_ready, 1)
                if isinstance(r, int) and r == 0 and k > FIRST + ET // SRC_PER:
                    w = k - FIRST - ET // SRC_PER - 1
                    for t in range(w * ET // SRC_SLOTS, (w + 1) * ET // SRC_SLOTS):
                        act.wait_ge(src_shift_ready, 1)
                        nc.scalar.activation(x1[0:EP, t, :], x1[0:EP, t, :], ACT.Identity,
                                             scale=src_rstd[0:EP, t:t + 1], bias=src_shift[0:EP, t:t + 1]) \
                            .then_inc(x1_ready, 1)
                if part in ("set0", "set1"):
                    if part == "set0" and k == FIRST:
                        act.wait_ge(table_loaded, 32)
                        act.wait_ge(x1_ready, ET)
                    for j, path, number in path_numbers(r, k, part):
                        i1 = load_segment(act, path, 0)
                        act.wait_ge(prod_free, number + 1)
                        nc.scalar.activation(prod[j % PB][0:EP, :, :],
                                             x1[0:EP, set_tiles(part), bass.ds(i1, EXTENT)],
                                             ACT.Copy, scale=coef[0:EP, bass.ds(path, 1)]).then_inc(scaled, 1)
                if live(r, k - L_HT):
                    act.wait_ge(HT_ready, tile(r, k - L_HT + 1))
                    if live(r, k - L_HT - 2):
                        act.wait_ge(O_ready, tile(r, k - L_HT - 1))
                    nc.scalar.activation(hT_hi[k % 2][:, :], HT[:, 0:HID], ACT.Copy).then_inc(hT_hi_ready, 1)
                t, j = sum_tile(r, k, part)
                if t is not None:
                    act.wait_ge(comb_ready, t + 1)
                    if part == "set1" and k == FIRST:
                        act.wait_ge(bias_moved, 16)
                    if part == "set1" or t == SET:
                        act.wait_ge(summed, t * 16 + 16)
                    else:
                        act.wait_ge(summed, t * 16)
                    nc.scalar.activation(moved[j][0:EP, :], C[0:EP, :], ACT.Copy).then_inc(C_free, 1)
                if live(r, k - L_SCALE):
                    act.wait_ge(hid_in_ready, tile(r, k - L_SCALE + 1))
                    nc.scalar.activation(hid[k % 2][:, :, :], hid[k % 2][:, :, :], ACT.Gelu).then_inc(hid_ready, 1)

            rounds(act, slot)

        @block.vector
        def _(dve):
            dve.wait_ge(col_mean, 1)
            for c in range(DC):
                last = nc.vector.tensor_tensor(w_raw[:, c, :], w_raw[:, c, :], U[0][:, 0:WC], ALU.subtract)
            last.then_inc(w_centered, 1)
            dve.wait_ge(w_rounded, 1)
            nc.vector.tensor_tensor(w_lo[:, :, :], w_raw, w_hi[:, :, :].bitcast(F32), ALU.subtract).then_inc(w_ready, 1)
            dve.wait_ge(w_rounded, 2)
            for h in range(HC):
                last = nc.vector.tensor_tensor(w2_lo[:, h, :], w2_raw[h], w2_hi[:, h, :].bitcast(F32), ALU.subtract)
            last.then_inc(w_ready, 1)
            dve.wait_ge(bias_hi_made, 1)
            nc.vector.tensor_tensor(bias_lo, C[0:1, :], bias_rows[0:1, :].bitcast(F32), ALU.subtract) \
                .then_inc(C_free, 1)

            def repeats_of(t):
                if t == 0:
                    dve.wait_ge(index_loaded, 32)
                    dve.wait_ge(all_dst_loaded, 16)
                    dve.wait_ge(pool_const, 4)
                    nc.vector.tensor_copy(dst_f[0:EP, :], dst_i[0:EP, :]).then_inc(dst_made, 1)
                    nc.vector.tensor_copy(spare_f[:, :], spare_i[:, :]).then_inc(dst_made, 1)
                    dve.wait_ge(dst_made, 2)
                nc.vector.tensor_scalar(same[0:EP, t, :], all_dst[0:EP, :, t], dst_f[0:EP, t:t + 1], None,
                                        ALU.is_equal).then_inc(eq_made, 1)
                dve.wait_ge(eq_made, 2 * t + 1)
                nc.vector.scalar_tensor_tensor(out=scratch, in0=same[0:EP, t, :], scalar=1.0,
                                               in1=later[0:EP, 0:EP], op0=ALU.mult, op1=ALU.mult,
                                               accum_out=repeats[0:EP, t:t + 1]).then_inc(eq_made, 1)

            def leaders():
                dve.wait_ge(eq_made, 2 * ET)
                nc.vector.tensor_scalar(away[0:EP, :], dst_f[0:EP, :], -1.0, spare_f[0:EP, 0:1],
                                        ALU.mult, ALU.add).then_inc(lead_step, 1)
                dve.wait_ge(lead_step, 1)
                nc.vector.scalar_tensor_tensor(out=away[0:EP, :], in0=repeats[0:EP, :], scalar=0.0,
                                               in1=away[0:EP, :], op0=ALU.is_gt, op1=ALU.mult) \
                    .then_inc(lead_step, 1)
                dve.wait_ge(lead_step, 2)
                nc.vector.tensor_tensor(lead_i[0:EP, :], away[0:EP, :], dst_f[0:EP, :], ALU.add) \
                    .then_inc(lead_ready, 1)

            def slot(r, k, part):
                m = k - L_FINAL
                a = k - L_SCALE
                pairs = r * PAIRS + k // 2
                c = a % 4
                if live(r, k):
                    dve.wait_ge(stats_made, tile(r, k + 1))
                if k % 2 == 0 and live(r, a):
                    dve.wait_ge(U_ready, tile(r, k))
                if live(r, m):
                    dve.wait_ge(O_ready, tile(r, m + 1))
                    if isinstance(r, int) and r * RING + m >= MAIN + ORING:
                        dve.wait_ge(scattered, 16 * (r * RING + m - MAIN - ORING + 1))
                    elif live(r, m - ORING):
                        dve.wait_ge(stored[m % ORING // 2], (r * (RING // ORING) + m // ORING) * 16)
                    nc.vector.tensor_tensor(outs[:, m % ORING, :], O[:, :], rows[:, m % RING, :], ALU.add) \
                        .then_inc(final_ready, 1)
                if live(r, k):
                    nc.vector.bn_aggr(mean_var[:, k % 4, :], stats[:, k % 4, :]).then_inc(var_ready, 1)
                if k % 2 == 0 and live(r, a):
                    nc.vector.max(top8[:, c, :], U[c][:, HID:WC])
                    nc.vector.max(top8[:, c + 1, :], U[c + 1][:, HID:WC]).then_inc(top_made, 1)
                    dve.wait_ge(top_made, pairs)
                    nc.vector.tensor_tensor(gap[:, c:c + 2], top8[:, c:c + 2, 0], top8[:, c:c + 2, 1],
                                            ALU.subtract).then_inc(gap_made, 1)
                    dve.wait_ge(gap_made, pairs)
                    dve.wait_ge(rstd_ready, pairs)
                    nc.vector.tensor_tensor(half_gap[:, c:c + 2], gap[:, c:c + 2], half_rstd[:, c:c + 2],
                                            ALU.mult).then_inc(half_gap_ready, 1)
                if live(r, k + 1):
                    dve.wait_ge(yT_hi_ready, tile(r, k + 2))
                    if live(r, k - 1):
                        dve.wait_ge(U_ready, tile(r, k))
                    nc.vector.tensor_tensor(yT_lo[(k + 1) % 2][:, :], yT[:, :],
                                            yT_hi[(k + 1) % 2][:, :].bitcast(F32), ALU.subtract) \
                        .then_inc(yT_lo_ready, 1)
                t, j = sum_tile(r, k, part)
                if t is not None:
                    dve.wait_ge(C_free, t + 1)
                    nc.vector.tensor_copy(same_now[0:EP, :], same[0:EP, bass.ds(t, 1), :]
                                          .rearrange("p a e -> p (a e)")).then_inc(same_ready, 1)
                if part in ("set0", "set1") and k > FIRST:
                    if part == "set0" and k == FIRST + 1:
                        dve.wait_ge(table_loaded, 32)
                    for j, path, number in path_numbers(r, k - 1, part):
                        i3 = load_segment(dve, path, 2)
                        dve.wait_ge(multiplied, number + 1)
                        dve.wait_ge(prod_free, number + PB)
                        sums = acc[0:EP, set_tiles(part), bass.ds(i3, EXTENT)]
                        nc.vector.tensor_tensor(sums, sums, prod[j % PB][0:EP, :, :], ALU.add).then_inc(prod_free, 1)
                if k % 2 == 0 and live(r, a):
                    dve.wait_ge(tanh_ready, pairs)
                    nc.vector.scalar_tensor_tensor(out=scale[:, c:c + 2, 0], in0=th[:, c:c + 2], scalar=1.0,
                                                   in1=half_rstd[:, c:c + 2], op0=ALU.add, op1=ALU.mult)
                    nc.vector.scalar_tensor_tensor(out=scale[:, c:c + 2, 1], in0=th[:, c:c + 2], scalar=1.0,
                                                   in1=half_rstd[:, c:c + 2], op0=ALU.subtract, op1=ALU.mult,
                                                   reverse0=True).then_inc(scale_ready, 1)
                if live(r, a):
                    dve.wait_ge(scale_ready, r * PAIRS + (k - 1) // 2 + (1 if k % 2 == 0 else 0)
                                if k % 2 else pairs)
                    if live(r, a - 2):
                        dve.wait_ge(hsum_ready, tile(r, a - 1))
                    for i in range(2):
                        last = nc.vector.scalar_tensor_tensor(out=hid[k % 2][:, i, :], in0=U[c][:, 0:HID],
                                                              scalar=scale[:, c, i:i + 1], in1=b1_bc[:, :],
                                                              op0=ALU.mult, op1=ALU.add)
                    last.then_inc(hid_in_ready, 1)
                if live(r, k - L_HT):
                    dve.wait_ge(hT_hi_ready, tile(r, k - L_HT + 1))
                    if live(r, k - L_HT - 2):
                        dve.wait_ge(O_ready, tile(r, k - L_HT - 1))
                    nc.vector.tensor_tensor(hT_lo[k % 2][:, :], HT[:, 0:HID], hT_hi[k % 2][:, :].bitcast(F32),
                                            ALU.subtract).then_inc(hT_lo_ready, 1)
                if live(r, k + 1):
                    c1 = (k + 1) % 4
                    wait_rows(dve, r, k + 1)
                    nc.vector.bn_stats(stats[:, c1, :], rows[:, (k + 1) % RING, :]).then_inc(stats_made, 1)
                if isinstance(r, int) and r == 0 and FIRST <= k < FIRST + ET // SRC_PER:
                    t = SRC_PER * (k - FIRST)
                    for i in range(SETS):
                        dve.wait_ge(x1_loaded[i], 16 * SET)
                    for i in range(SRC_PER):
                        last = nc.vector.bn_stats(src_stats[0:EP, t + i, :], x1[0:EP, t + i, :])
                    last.then_inc(src_stats_made, 1)
                    dve.wait_ge(src_stats_made, k - FIRST + 1)
                    for i in range(SRC_PER):
                        last = nc.vector.bn_aggr(src_mv[0:EP, t + i, :], src_stats[0:EP, t + i, :])
                    last.then_inc(src_var_ready, 1)
                if isinstance(r, int) and r == 0 and k == FIRST + ET // SRC_PER:
                    dve.wait_ge(src_rstd_ready, 1)
                    nc.vector.scalar_tensor_tensor(out=src_shift[0:EP, :], in0=src_mv[0:EP, :, 0], scalar=-1.0,
                                                   in1=src_rstd[0:EP, :], op0=ALU.mult, op1=ALU.mult) \
                        .then_inc(src_shift_ready, 1)
                if isinstance(r, int) and r == 0 and FIRST + ET // SRC_PER <= k < FIRST + 2 * ET // SRC_PER:
                    for i in range(SRC_PER):
                        repeats_of(SRC_PER * (k - FIRST) - ET + i)
                    if k == FIRST + 2 * ET // SRC_PER - 1:
                        leaders()

            rounds(dve, slot)

        @block.gpsimd
        def _(pool):
            nc.gpsimd.memset(mean_mat, 1.0 / D).then_inc(pool_const, 1)
            nc.gpsimd.memset(twos, 2.0)
            nc.gpsimd.memset(ident[:, :], 0.0)
            nc.gpsimd.memset(later, 0.0).then_inc(pool_const, 1)
            pool.wait_ge(pool_const, 2)
            nc.gpsimd.affine_select(out=ident[:, :], in_=ident[:, :], compare_op=ALU.not_equal, fill=1.0,
                                    base=0, pattern=[[-1, P]], channel_multiplier=1).then_inc(pool_const, 1)
            nc.gpsimd.affine_select(out=later, in_=later, compare_op=ALU.is_ge, fill=1.0,
                                    base=0, pattern=[[-1, P]], channel_multiplier=1)
            nc.gpsimd.iota(spare_i[:, :], pattern=[[0, 1]], base=N, channel_multiplier=1).then_inc(pool_const, 1)
            nc.gpsimd.memset(minus_half[:, :], -0.5)
            nc.gpsimd.memset(ones[:, :].bitcast(F32), 1.0)
            nc.gpsimd.memset(bias_rows[:, :].bitcast(F32), 0.0).then_inc(bias_zero, 1)

            pool.wait_ge(index_loaded, 32)
            for t in range(ET):
                nc.gpsimd.indirect_dma_start(
                    out=x1[0:EP, t, :], out_offset=None, in_=x,
                    in_offset=bass.IndirectOffsetOnAxis(ap=src_i[0:EP, t:t + 1], axis=0),
                ).then_inc(x1_loaded[t // SET], 16)
            pool.dma_start(y_rows[N:N + P, :], x[0:P, :]).then_inc(summed, 16)

            def slot(r, k, part):
                s = k - FIRST
                if isinstance(r, int) and r == 0 and s == 0:
                    nc.gpsimd.memset(acc[0:EP, dst_tiles:SET, :], 0.0)
                if isinstance(r, int) and r == 0 and s == 3:
                    nc.gpsimd.memset(acc[0:EP, SET:ET - 3, :], 0.0)
                if isinstance(r, int) and r == 0 and s == 6:
                    nc.gpsimd.memset(acc[0:EP, ET - 3:ET, :], 0.0)
                if isinstance(r, int) and r == 0 and s == RING - 1:
                    pool.wait_ge(eq_made, 2 * ET)
                    nc.gpsimd.memset(acc[0:EP, 0:dst_tiles, :], 0.0).then_inc(prod_free, PB)


                if part in ("set0", "set1"):
                    if part == "set0" and k == FIRST:
                        pool.wait_ge(attr_loaded, 32)
                        pool.wait_ge(table_loaded, 32)
                    if part == "set1" and k == FIRST:
                        pool.wait_ge(lead_ready, 1)
                        pool.wait_ge(y_filled, 16 * FILLS)
                        pool.wait_ge(summed, (r - SET1[0]) * (SET // 2) * 16 + 16)
                    for j, path, number in path_numbers(r, k, part):
                        i2 = load_segment(pool, path, 1)
                        pool.wait_ge(scaled, number + 1)
                        p = prod[j % PB][0:EP, :, :]
                        nc.gpsimd.tensor_tensor(p, p, x2[0:EP, set_tiles(part), bass.ds(i2, EXTENT)], ALU.mult) \
                            .then_inc(multiplied, 1)
                if part == "set1" and s == 0:
                    t = (r - SET1[0]) * (SET // 2)
                    nc.gpsimd.tensor_copy(put_i[0:EP, :], lead_i[0:EP, bass.ds(t, SET // 2)]) \
                        .then_inc(index_copied, 1)
                    pool.wait_ge(index_copied, r - SET1[0] + 1)

                t0, j0 = sum_tile(r, k - 1, part) if s >= 1 else (None, None)
                if t0 is not None:
                    pool.wait_ge(summed, t0 * 16 + 16)
                    pool.wait_ge(C_free, t0 + 2)
                if k % 2 and live(r, k):
                    pool.wait_ge(var_ready, tile(r, k + 1))
                    if live(r, k - 4):
                        pool.wait_ge(scale_ready, r * PAIRS + k // 2 - 1)
                if live(r, k - L_SCALE):
                    pool.wait_ge(hid_ready, tile(r, k - L_SCALE + 1))
                    if live(r, k - L_SCALE - 2):
                        pool.wait_ge(HT_ready, tile(r, k - L_SCALE - 1))
                    nc.gpsimd.tensor_tensor(hsum[k % 2][:, :], hid[k % 2][:, 0, :], hid[k % 2][:, 1, :], ALU.add) \
                        .then_inc(hsum_ready, 1)
                if k % 2 and live(r, k):
                    c = (k - 1) % 4
                    nc.gpsimd.tensor_scalar(var4[:, c:c + 2], mean_var[:, c:c + 2, 1], EPS, 4.0,
                                            ALU.add, ALU.mult).then_inc(var4_made, 1)
                    pool.wait_ge(var4_made, r * PAIRS + k // 2 + 1)
                    nc.gpsimd.tensor_tensor(half_rstd[:, c:c + 2], var4[:, c:c + 2], minus_half[:, 0:2],
                                            ALU.pow).then_inc(rstd_ready, 1)

                if isinstance(r, int) and r == 0 and k == FIRST + ET // SRC_PER - 1:
                    pool.wait_ge(src_var_ready, ET // SRC_PER)
                    nc.gpsimd.tensor_scalar(src_rstd[0:EP, :], src_mv[0:EP, :, 1], EPS, 1.0,
                                            ALU.add, ALU.mult).then_inc(src_rstd_step, 1)
                    pool.wait_ge(src_rstd_step, 1)
                    nc.gpsimd.tensor_tensor(src_rstd[0:EP, :], src_rstd[0:EP, :], minus_half[0:EP, :],
                                            ALU.pow).then_inc(src_rstd_ready, 1)
                if t0 is not None:
                    where = put_i[0:EP, s // 2:s // 2 + 1] if part == "set1" else lead_i[0:EP, t0:t0 + 1]
                    nc.gpsimd.indirect_dma_start(
                        out=y_rows, out_offset=bass.IndirectOffsetOnAxis(ap=where, axis=0),
                        in_=moved[j0][0:EP, :], in_offset=None, compute_op=ALU.add).then_inc(summed, 16)
                if isinstance(r, int) and MAIN <= r * RING + k + L_GATHER < TILES:
                    m = r * RING + k + L_GATHER
                    if m == MAIN:
                        pool.wait_ge(summed, 16 * ET + 16)
                    pool.wait_ge(final_ready, m - RING + 1)
                    nc.gpsimd.indirect_dma_start(
                        out=rows[0:EP, m % RING, :], out_offset=None, in_=y_rows,
                        in_offset=bass.IndirectOffsetOnAxis(ap=dst_i[0:EP, m - MAIN:m - MAIN + 1], axis=0),
                    ).then_inc(edge_loaded[m % RING], 16)
                if isinstance(r, int) and MAIN <= r * RING + k - L_STORE < TILES:
                    m = r * RING + k - L_STORE
                    if m == MAIN:
                        for i in range(2):
                            pool.wait_ge(stored[i], 16 * (MAIN_PAIRS // 2))
                    pool.wait_ge(final_ready, m + 1)
                    if m > MAIN:
                        pool.wait_ge(scattered, 16 * (m - MAIN))
                    nc.gpsimd.indirect_dma_start(
                        out=out, out_offset=bass.IndirectOffsetOnAxis(ap=lead_i[0:EP, m - MAIN:m - MAIN + 1], axis=0),
                        in_=outs[0:EP, m % ORING, :], in_offset=None,
                        bounds_check=N - 1, oob_is_err=False).then_inc(scattered, 16)

            rounds(pool, slot)
            pool.wait_ge(scattered, 16 * ET)

        @block.tensor
        def _(pe):
            pe.wait_ge(pool_const, 4)
            pe.wait_ge(w_loaded, 16 * (DC + 1))
            for c in range(DC):
                last = nc.tensor.matmul(U[0][:, 0:WC], mean_mat, w_raw[:, c, :], start=(c == 0), stop=(c == DC - 1))
            last.then_inc(col_mean, 1)
            pe.wait_ge(bias_loaded, 32)
            nc.tensor.matmul(C[:, :], twos[0:EXPERTS, :], b2_raw, start=True, stop=True).then_inc(bias_sum, 1)

            def slot(r, k, part):
                if live(r, k + 1):
                    wait_rows(pe, r, k + 1)
                    if live(r, k):
                        pe.wait_ge(yT_lo_ready, tile(r, k + 1))
                    for c in range(DC):
                        last = nc.tensor.transpose(yT[:, c * P:(c + 1) * P],
                                                   rows[:, (k + 1) % RING, c * P:(c + 1) * P], ident[:, :])
                    last.then_inc(yT_ready, 1)
                if live(r, k):
                    if isinstance(r, int) and r == 0 and k == 0:
                        pe.wait_ge(w_ready, 1)
                        pe.wait_ge(yT_lo_ready, 1)
                    if not live(r, k + 1):
                        pe.wait_ge(yT_lo_ready, tile(r, k + 1))
                    if live(r, k - 4):
                        pe.wait_ge(hid_in_ready, tile(r, k - 3))
                    u = U[k % 4][:, 0:WC]
                    hi, lo = yT_hi[k % 2], yT_lo[k % 2]
                    for c in range(DC):
                        cc = slice(c * P, (c + 1) * P)
                        nc.tensor.matmul(u, hi[:, cc], w_hi[:, c, :], start=(c == 0), stop=False)
                        nc.tensor.matmul(u, hi[:, cc], w_lo[:, c, :], start=False, stop=False)
                        last = nc.tensor.matmul(u, lo[:, cc], w_hi[:, c, :], start=False, stop=(c == DC - 1))
                    last.then_inc(U_ready, 1)
                t, j = sum_tile(r, k, part)
                if t is not None:
                    if k == FIRST:
                        pe.wait_ge(prod_free, PB + (NP if part == "set1" else 2 * NP))
                    pe.wait_ge(same_ready, t + 1)
                    pe.wait_ge(C_free, t + 1)
                    nc.tensor.matmul(C[0:EP, :], same_now[0:EP, :],
                                     acc[0:EP, bass.ds(t, 1), :].rearrange("p a d -> p (a d)"),
                                     start=True, stop=True).then_inc(comb_ready, 1)
                m = k - L_HT
                if live(r, m):
                    pe.wait_ge(hsum_ready, tile(r, m + 1))
                    if live(r, m - 1):
                        pe.wait_ge(hT_lo_ready, tile(r, m))
                    for h in range(HC):
                        last = nc.tensor.transpose(HT[:, h * P:(h + 1) * P], hsum[m % 2][:, h * P:(h + 1) * P],
                                                   ident[:, :])
                    last.then_inc(HT_ready, 1)
                m = k - L_DOWN
                if live(r, m):
                    if isinstance(r, int) and r * RING + m == 0:
                        pe.wait_ge(bias_moved, 16)
                        pe.wait_ge(w_ready, 2)
                    if live(r, m - 1):
                        pe.wait_ge(final_ready, tile(r, m))
                    nc.tensor.matmul(O[:, :], ones[:, :], bias_rows[:, :], start=True, stop=False)
                    pe.wait_ge(hT_lo_ready, tile(r, m + 1))
                    hi, lo = hT_hi[m % 2], hT_lo[m % 2]
                    for h in range(HC):
                        hh = slice(h * P, (h + 1) * P)
                        nc.tensor.matmul(O[:, :], hi[:, hh], w2_hi[:, h, :], start=False, stop=False)
                        nc.tensor.matmul(O[:, :], hi[:, hh], w2_lo[:, h, :], start=False, stop=False)
                        last = nc.tensor.matmul(O[:, :], lo[:, hh], w2_hi[:, h, :], start=False, stop=(h == HC - 1))
                    last.then_inc(O_ready, 1)

            rounds(pe, slot)


_INS = ["x", "src", "dst", "edge_attr_512", "L0_gnn_path_coeffs", "L0_gnn_path_indices",
        "L0_ffn_Wg", "L0_ffn_W1", "L0_ffn_b1", "L0_ffn_W2", "L0_ffn_b2"]


def kernel(**inputs):
    import numpy as _np
    import concourse.bacc as _bacc
    from concourse import mybir as _mybir
    from concourse.bass_utils import run_bass_kernel_spmd as _run

    nc = _bacc.Bacc("TRN2", target_bir_lowering=False, num_devices=1)
    arrays, args = {}, []
    for name in _INS:
        a = _np.ascontiguousarray(inputs[name])
        arrays[f"in_{name}"] = a
        args.append(nc.dram_tensor(f"in_{name}", a.shape, _mybir.dt.from_np(a.dtype), kind="ExternalInput").ap())
    shape = inputs["x"].shape
    args.append(nc.dram_tensor("out_rows", shape, _mybir.dt.float32, kind="ExternalOutput").ap())
    gnn_ffn_kernel(nc, *args)
    r = _run(nc, [arrays], core_ids=[0])
    return r.results[0]["out_rows"]
```

```python
import numpy as np
import concourse.bass as bass
from concourse import mybir
from contextlib import ExitStack


def gnn_ffn_kernel(nc, x, src, dst, edge_attr, path_coeffs, path_indices, Wg, W1, b1, W2, b2, out):
    F32 = mybir.dt.float32
    F32R = mybir.dt.float32r
    BF16 = mybir.dt.bfloat16
    U8 = mybir.dt.uint8
    I32 = mybir.dt.int32
    ALU = mybir.AluOpType
    ACT = mybir.ActivationFunctionType

    N, D = x.shape
    NE = src.shape[0]
    NP = path_coeffs.shape[0]
    EXPERTS, _, DFF = W1.shape
    HID = EXPERTS * DFF
    WC = HID + EXPERTS
    EXTENT = 32
    NSEG = D // EXTENT
    EPS = 1e-5
    P = 128
    DC = D // P
    HC = HID // P

    ET = 20
    EP = NE // ET
    assert EP * ET == NE and EP <= P
    SET = ET // 2
    SETS = 2

    RING = 12
    PAIRS = RING // 2
    ORING = 4
    FIRST = 4
    MAIN_PAIRS = -(-N // (2 * P))
    MAIN = 2 * MAIN_PAIRS
    TILES = MAIN + ET
    ROUNDS = (TILES - FIRST) // RING
    assert FIRST + ROUNDS * RING == TILES and MAIN % ORING == 0
    L_SCALE, L_SUM, L_HT, L_DOWN, L_FINAL, L_STORE, L_GATHER = 2, 3, 4, 4, 5, 6, 5
    SET0, SET1, SUM1 = (1, 3), (3, 5), 5
    PPR = NP // 2
    PER_SLOT = [3] * 10 + [2, 0]
    PB = 4
    SRC_PER = 4
    SRC_SLOTS = RING - ET // SRC_PER - 1
    FILLS_LOOPED = 10
    FILLS = RING + FILLS_LOOPED * (SET0[1] - SET0[0])
    FILL = N * D // FILLS
    assert FILL * FILLS == N * D and FILL % 16 == 0
    assert sum(PER_SLOT) == PPR and len(PER_SLOT) == RING

    y_rows = nc.dram_tensor("y_rows", (N + P, D), F32, kind="Internal").ap()
    y_flat = y_rows.rearrange("n d -> (n d)")
    x_flat = x.rearrange("n d -> (n d)")

    def pair_rows(dram, q):
        base = q * 2 * P
        if isinstance(q, int):
            base = min(base, N - 2 * P)
        return dram[bass.ds(base, 2 * P), :].rearrange("(p j) d -> p j d", j=2)

    ctx = ExitStack()
    with ctx:
        def sb(name, shape, dt=F32):
            return ctx.enter_context(nc.sbuf_tensor(name, shape, dt))

        def pb(name, shape):
            return ctx.enter_context(nc.psum_tensor(name, shape, F32))

        def sem(name):
            return ctx.enter_context(nc.semaphore(name))

        rows = sb("rows", [P, RING, D])
        outs = sb("outs", [P, ORING, D])
        x1 = sb("x1", [P, ET, D])
        x2 = sb("x2", [P, ET, D])
        acc = sb("acc", [P, ET, D])
        same = sb("same", [P, ET, EP], U8)
        same_now = sb("same_now", [P, EP])
        prod = [sb(f"prod{i}", [P, SET, EXTENT]) for i in range(PB)]
        yT_hi = [sb(f"yT_hi{i}", [P, D], F32R) for i in range(2)]
        yT_lo = [sb(f"yT_lo{i}", [P, D], F32R) for i in range(2)]
        w_hi = sb("w_hi", [P, DC, WC], F32R)
        w_lo = sb("w_lo", [P, DC, WC], F32R)
        w2_hi = sb("w2_hi", [P, HC, D], F32R)
        w2_lo = sb("w2_lo", [P, HC, D], F32R)
        hid = [sb(f"hid{i}", [P, 2, HID]) for i in range(2)]
        hsum = [sb(f"hsum{i}", [P, HID]) for i in range(2)]
        hT_hi = [sb(f"hT_hi{i}", [P, HID], F32R) for i in range(2)]
        hT_lo = [sb(f"hT_lo{i}", [P, HID], F32R) for i in range(2)]
        moved = [sb(f"moved{i}", [P, D]) for i in range(2)]
        b1_bc = sb("b1_bc", [P, HID])
        bias_rows = sb("bias_rows", [P, D], F32R)
        ones = sb("ones", [P, P], F32R)
        ident = sb("ident", [P, P])
        coef = sb("coef", [P, NP])
        table = sb("table", [1, NP * 3], I32)
        src_i = sb("src_i", [P, ET], I32)
        dst_i = sb("dst_i", [P, ET], I32)
        dst_f = sb("dst_f", [P, ET])
        repeats = sb("repeats", [P, ET])
        away = sb("away", [P, ET])
        lead_i = sb("lead_i", [P, ET], I32)
        spare_i = sb("spare_i", [P, 1], I32)
        spare_f = sb("spare_f", [P, 1])
        put_i = sb("put_i", [P, SET // 2], I32)
        src_stats = sb("src_stats", [P, ET, 6])
        src_mv = sb("src_mv", [P, ET, 2])
        src_rstd = sb("src_rstd", [P, ET])
        src_shift = sb("src_shift", [P, ET])
        unused = sb("unused", [P, D], BF16)
        minus_mean = sb("minus_mean", [P, 4])
        squares = sb("squares", [P, 4])
        var4 = sb("var4", [P, 4])
        half_rstd = sb("half_rstd", [P, 4])
        minus_half = sb("minus_half", [P, ET])
        top8 = sb("top8", [P, 4, 8])
        half_gap = sb("half_gap", [P, 4])
        th = sb("th", [P, 4])
        scale = sb("scale", [P, 4, 2])

        yT = pb("yT", [P, D])
        U = [pb(f"U{i}", [P, 512]) for i in range(4)]
        HT = pb("HT", [P, 512])
        O = pb("O", [P, D])
        C = pb("C", [P, D])

        w_raw = outs[:, :, :].rearrange("p a d -> p (a d)")[:, 0:DC * WC].rearrange("p (c n) -> p c n", c=DC)
        w2_raw = [hid[h][:, :, :].rearrange("p a f -> p (a f)") for h in range(HC)]
        b2_raw = moved[0][0:EXPERTS, :]
        bias_lo = moved[1][0:1, :].bitcast(F32R)
        mean_mat = prod[0][:, :, :].rearrange("p t u -> p (t u)")[:, 0:P]
        twos = prod[1][:, :, :].rearrange("p t u -> p (t u)")[:, 0:P]
        all_dst = acc[:, :, :].rearrange("p t d -> p (t d)")[:, 0:NE].bitcast(I32) \
            .rearrange("p (e t) -> p e t", t=ET)
        dst_tiles = -(-NE // D)
        later = prod[3][:, :, :].rearrange("p t u -> p (t u)")[:, 0:P]
        scratch = prod[2][:, :, :].rearrange("p t u -> p (t u)")[0:EP, 0:EP]

        x_loaded = [sem(f"x_loaded{i}") for i in range(PAIRS)]
        edge_loaded = [sem(f"edge_loaded{i}") for i in range(RING)]
        w_loaded = sem("w_loaded")
        w2_loaded = sem("w2_loaded")
        bias_loaded = sem("bias_loaded")
        index_loaded = sem("index_loaded")
        all_dst_loaded = sem("all_dst_loaded")
        table_loaded = sem("table_loaded")
        attr_loaded = sem("attr_loaded")
        x1_loaded = [sem(f"x1_loaded{i}") for i in range(SETS)]
        pool_const = sem("pool_const")
        const_ready = sem("const_ready")
        col_mean = sem("col_mean")
        w_centered = sem("w_centered")
        w_rounded = sem("w_rounded")
        w_ready = sem("w_ready")
        bias_sum = sem("bias_sum")
        bias_hi_made = sem("bias_hi_made")
        bias_moved = sem("bias_moved")
        bias_zero = sem("bias_zero")
        src_stats_made = sem("src_stats_made")
        src_var_ready = sem("src_var_ready")
        src_rstd_step = sem("src_rstd_step")
        src_rstd_ready = sem("src_rstd_ready")
        src_shift_ready = sem("src_shift_ready")
        x1_ready = sem("x1_ready")
        dst_made = sem("dst_made")
        eq_made = sem("eq_made")
        lead_step = sem("lead_step")
        lead_ready = sem("lead_ready")
        multiplied = sem("multiplied")
        prod_free = sem("prod_free")
        index_copied = sem("index_copied")
        y_filled = sem("y_filled")
        same_ready = sem("same_ready")
        comb_ready = sem("comb_ready")
        C_free = sem("C_free")
        summed = sem("summed")
        yT_ready = sem("yT_ready")
        yT_hi_ready = sem("yT_hi_ready")
        yT_lo_ready = sem("yT_lo_ready")
        U_ready = sem("U_ready")
        mean_made = sem("mean_made")
        squares_ready = sem("squares_ready")
        var4_made = sem("var4_made")
        rstd_ready = sem("rstd_ready")
        top_made = sem("top_made")
        half_gap_ready = sem("half_gap_ready")
        tanh_ready = sem("tanh_ready")
        scale_ready = sem("scale_ready")
        hid_in_ready = sem("hid_in_ready")
        hid_ready = sem("hid_ready")
        hsum_ready = sem("hsum_ready")
        HT_ready = sem("HT_ready")
        hT_hi_ready = sem("hT_hi_ready")
        hT_lo_ready = sem("hT_lo_ready")
        O_ready = sem("O_ready")
        final_ready = sem("final_ready")
        stored = [sem(f"stored{i}") for i in range(ORING // 2)]
        scattered = sem("scattered")

        block = ctx.enter_context(nc.Block())

        def rounds(eng, slot):
            for k in range(-1, FIRST):
                slot(0, k, None)
            for k in range(FIRST, FIRST + RING):
                slot(0, k, None)
            for part, (r0, r1) in (("set0", SET0), ("set1", SET1)):
                with eng.Fori(r0, r1) as r:
                    for k in range(FIRST, FIRST + RING):
                        slot(r, k, part)
            for r in range(SUM1, ROUNDS):
                for k in range(FIRST, FIRST + RING):
                    slot(r, k, "sum1" if r == SUM1 else None)
            for k in range(FIRST, FIRST + L_STORE + 1):
                slot(ROUNDS, k, None)

        def live(r, k):
            return 0 <= r * RING + k < TILES if isinstance(r, int) else True

        def tile(r, k):
            return r * RING + k

        def is_edge(r, k):
            return isinstance(r, int) and r * RING + k >= MAIN

        def wait_rows(eng, r, k):
            if is_edge(r, k):
                eng.wait_ge(edge_loaded[k % RING], 16 * ((r * RING + k - MAIN) // RING + 1))
            else:
                eng.wait_ge(x_loaded[k % RING // 2], (r + k // RING) * 16 + 16)

        def slot_paths(k):
            first = sum(PER_SLOT[:k - FIRST])
            return range(first, first + PER_SLOT[k - FIRST])

        def set_tiles(part):
            return slice(0, SET) if part == "set0" else slice(SET, ET)

        def path_numbers(r, k, part):
            first = (r - (SET0 if part == "set0" else SET1)[0]) * PPR
            return [(j, first + j, (r - SET0[0]) * PPR + j) for j in slot_paths(k)]

        def load_segments(engine, paths):
            if not paths:
                return []
            _, values = nc.values_load_multi_w_load_instructions(
                table[0:1, bass.ds(paths[0][1] * 3, 3 * len(paths))], engines=(engine,), min_val=0, max_val=NSEG - 1,
                skip_runtime_bounds_check_because="the segment numbers of a path are below NSEG")
            return [tuple(v * EXTENT for v in values[3 * i:3 * i + 3]) for i in range(len(paths))]

        def sum_tile(r, k, part):
            s = k - FIRST
            if part == "set1" and s % 2 == 0 and s // 2 < SET // 2:
                return (r - SET1[0]) * (SET // 2) + s // 2, s // 2 % 2
            if part == "sum1" and 0 <= s < SET:
                return SET + s, s % 2
            return None, None

        @block.sync
        def _(sp):
            def load(q, i):
                sp.dma_start(rows[:, 2 * i:2 * i + 2, :], pair_rows(x, q)).then_inc(x_loaded[i], 16)

            def store(q, i):
                sp.dma_start(pair_rows(out, q), outs[:, 2 * (i % 2):2 * (i % 2) + 2, :]) \
                    .then_inc(stored[i % 2], 16)

            load(0, 0)
            for c in range(DC):
                sp.dma_start(w_raw[:, c, 0:HID].rearrange("p (e f) -> p e f", e=EXPERTS),
                             W1[:, c * P:(c + 1) * P, :].rearrange("e p f -> p e f")).then_inc(w_loaded, 16)
            sp.dma_start(w_raw[:, :, HID:WC], Wg.rearrange("(c p) e -> p c e", p=P)).then_inc(w_loaded, 16)
            for q in range(1, PAIRS):
                load(q, q)
            loops = (MAIN_PAIRS - PAIRS) // PAIRS
            with sp.Fori(0, loops) as r:
                for i in range(PAIRS):
                    q = r * PAIRS + i
                    sp.wait_ge(final_ready, q * 2 + 2)
                    store(q, i)
                    load(q + PAIRS, i)
            for q in range(loops * PAIRS, MAIN_PAIRS):
                sp.wait_ge(final_ready, 2 * q + 2)
                if q == MAIN_PAIRS - 1:
                    sp.wait_ge(stored[(q - 1) % 2], 16 * ((q - 1) // 2 + 1))
                store(q, q % PAIRS)
                if q + PAIRS < MAIN_PAIRS:
                    load(q + PAIRS, q % PAIRS)
            for i in range(2):
                sp.wait_ge(stored[i], 16 * (MAIN_PAIRS // 2))

        @block.scalar
        def _(act):
            act.dma_start(src_i[0:EP, :], src.rearrange("(p t) -> p t", t=ET)).then_inc(index_loaded, 16)
            act.dma_start(dst_i[0:EP, :], dst.rearrange("(p t) -> p t", t=ET)).then_inc(index_loaded, 16)
            act.dma_start(b2_raw, b2).then_inc(bias_loaded, 16)
            act.dma_start(b1_bc[:, :], b1.rearrange("e f -> (e f)").partition_broadcast(P)).then_inc(bias_loaded, 16)
            for h in range(HC):
                act.dma_start(w2_raw[h], W2.rearrange("e f d -> (e f) d")[h * P:(h + 1) * P, :]) \
                    .then_inc(w2_loaded, 16)
            act.dma_start(all_dst[0:EP, :, :], dst.rearrange("(p t) -> p t", t=ET).partition_broadcast(EP)) \
                .then_inc(all_dst_loaded, 16)
            act.dma_start(table[0:1, :], path_indices.rearrange("n c -> (n c)").unsqueeze(0)) \
                .then_inc(table_loaded, 16)
            act.dma_start(coef[:, :], path_coeffs.partition_broadcast(P)).then_inc(table_loaded, 16)
            attr = edge_attr.rearrange("(p t) d -> p (t d)", t=ET)
            even = EP // 8 * 8
            for lo, hi in ((0, even), (even, EP)):
                act.dma_start(x2[lo:hi, :, :].rearrange("p t d -> p (t d)"), attr[lo:hi, :]) \
                    .then_inc(attr_loaded, 16)

            act.wait_ge(w_centered, 1)
            nc.scalar.activation(w_hi[:, :, :], w_raw, ACT.Copy).then_inc(w_rounded, 1)
            act.wait_ge(w2_loaded, 16 * HC)
            for h in range(HC):
                last = nc.scalar.activation(w2_hi[:, h, :], w2_raw[h], ACT.Copy)
            last.then_inc(w_rounded, 1)
            act.wait_ge(bias_sum, 1)
            act.wait_ge(bias_zero, 1)
            nc.scalar.activation(bias_rows[0:1, :], C[0:1, :], ACT.Copy).then_inc(bias_hi_made, 1)
            act.wait_ge(C_free, 1)
            act.dma_start(bias_rows[1:2, :].bitcast(F32), bias_lo.bitcast(F32)).then_inc(bias_moved, 16)

            def slot(r, k, part):
                s = k - FIRST
                if part == "set0" and s < FILLS_LOOPED or isinstance(r, int) and r == 0 and 0 <= s < RING:
                    f = s if part is None else RING + (r - SET0[0]) * FILLS_LOOPED + s
                    act.dma_start(y_flat[bass.ds(f * FILL, FILL)].rearrange("(a r) -> a r", a=16),
                                  x_flat[bass.ds(f * FILL, FILL)].rearrange("(a r) -> a r", a=16)) \
                        .then_inc(y_filled, 16)
                if live(r, k + 1):
                    c = (k + 1) % 4
                    wait_rows(act, r, k + 1)
                    if live(r, k):
                        act.wait_ge(squares_ready, tile(r, k + 1))
                    nc.scalar.activation(unused[:, :], rows[:, (k + 1) % RING, :], ACT.Copy, scale=-1.0 / D,
                                         accum_out=minus_mean[:, c:c + 1]).then_inc(mean_made, 1)
                if live(r, k + 1):
                    act.wait_ge(yT_ready, tile(r, k + 2))
                    if live(r, k - 1):
                        act.wait_ge(U_ready, tile(r, k))
                    nc.scalar.activation(yT_hi[(k + 1) % 2][:, :], yT[:, :], ACT.Copy).then_inc(yT_hi_ready, 1)
                if live(r, k - L_HT):
                    act.wait_ge(HT_ready, tile(r, k - L_HT + 1))
                    if live(r, k - L_HT - 2):
                        act.wait_ge(O_ready, tile(r, k - L_HT - 1))
                    nc.scalar.activation(hT_hi[k % 2][:, :], HT[:, 0:HID], ACT.Copy).then_inc(hT_hi_ready, 1)
                t, j = sum_tile(r, k - 1, part)
                if t is not None:
                    act.wait_ge(comb_ready, t + 1)
                    if part == "set1" and k == FIRST + 1:
                        act.wait_ge(bias_moved, 16)
                    if part == "set1" or t == SET:
                        act.wait_ge(summed, t * 16 + 16)
                    else:
                        act.wait_ge(summed, t * 16)
                    nc.scalar.activation(moved[j][0:EP, :], C[0:EP, :], ACT.Copy).then_inc(C_free, 1)
                if live(r, k + 1):
                    c = (k + 1) % 4
                    act.wait_ge(mean_made, tile(r, k + 2))
                    if live(r, k - 3):
                        act.wait_ge(var4_made, r * PAIRS + (k - 1) // 2)
                    nc.scalar.activation(unused[:, :], rows[:, (k + 1) % RING, :], ACT.Square,
                                         bias=minus_mean[:, c:c + 1],
                                         accum_out=squares[:, c:c + 1]).then_inc(squares_ready, 1)
                if live(r, k - L_SCALE):
                    act.wait_ge(hid_in_ready, tile(r, k - L_SCALE + 1))
                    nc.scalar.activation(hid[k % 2][:, :, :], hid[k % 2][:, :, :], ACT.Gelu).then_inc(hid_ready, 1)
                if isinstance(r, int) and r == 0 and k > FIRST + ET // SRC_PER:
                    w = k - FIRST - ET // SRC_PER - 1
                    for t in range(w * ET // SRC_SLOTS, (w + 1) * ET // SRC_SLOTS):
                        act.wait_ge(src_shift_ready, 1)
                        nc.scalar.activation(x1[0:EP, t, :], x1[0:EP, t, :], ACT.Identity,
                                             scale=src_rstd[0:EP, t:t + 1], bias=src_shift[0:EP, t:t + 1]) \
                            .then_inc(x1_ready, 1)
                if k % 2 and live(r, k):
                    act.wait_ge(half_gap_ready, r * PAIRS + (k + 1) // 2)
                    c = (k - 1) % 4
                    nc.scalar.activation(th[:, c:c + 2], half_gap[:, c:c + 2], ACT.Tanh).then_inc(tanh_ready, 1)

            rounds(act, slot)

        @block.vector
        def _(dve):
            dve.wait_ge(col_mean, 1)
            for c in range(DC):
                last = nc.vector.tensor_tensor(w_raw[:, c, :], w_raw[:, c, :], U[0][:, 0:WC], ALU.subtract)
            last.then_inc(w_centered, 1)
            dve.wait_ge(w_rounded, 1)
            nc.vector.tensor_tensor(w_lo[:, :, :], w_raw, w_hi[:, :, :].bitcast(F32), ALU.subtract).then_inc(w_ready, 1)
            dve.wait_ge(w_rounded, 2)
            for h in range(HC):
                last = nc.vector.tensor_tensor(w2_lo[:, h, :], w2_raw[h], w2_hi[:, h, :].bitcast(F32), ALU.subtract)
            last.then_inc(w_ready, 1)
            dve.wait_ge(bias_hi_made, 1)
            nc.vector.tensor_tensor(bias_lo, C[0:1, :], bias_rows[0:1, :].bitcast(F32), ALU.subtract) \
                .then_inc(C_free, 1)

            def repeats_of(t):
                if t == 0:
                    dve.wait_ge(index_loaded, 32)
                    dve.wait_ge(all_dst_loaded, 16)
                    dve.wait_ge(pool_const, 4)
                    nc.vector.tensor_copy(dst_f[0:EP, :], dst_i[0:EP, :]).then_inc(dst_made, 1)
                    nc.vector.tensor_copy(spare_f[:, :], spare_i[:, :]).then_inc(dst_made, 1)
                    dve.wait_ge(dst_made, 2)
                nc.vector.tensor_scalar(same[0:EP, t, :], all_dst[0:EP, :, t], dst_f[0:EP, t:t + 1], None,
                                        ALU.is_equal).then_inc(eq_made, 1)
                dve.wait_ge(eq_made, 2 * t + 1)
                nc.vector.scalar_tensor_tensor(out=scratch, in0=same[0:EP, t, :], scalar=1.0,
                                               in1=later[0:EP, 0:EP], op0=ALU.mult, op1=ALU.mult,
                                               accum_out=repeats[0:EP, t:t + 1]).then_inc(eq_made, 1)

            def leaders():
                dve.wait_ge(eq_made, 2 * ET)
                nc.vector.tensor_scalar(away[0:EP, :], dst_f[0:EP, :], -1.0, spare_f[0:EP, 0:1],
                                        ALU.mult, ALU.add).then_inc(lead_step, 1)
                dve.wait_ge(lead_step, 1)
                nc.vector.scalar_tensor_tensor(out=away[0:EP, :], in0=repeats[0:EP, :], scalar=0.0,
                                               in1=away[0:EP, :], op0=ALU.is_gt, op1=ALU.mult) \
                    .then_inc(lead_step, 1)
                dve.wait_ge(lead_step, 2)
                nc.vector.tensor_tensor(lead_i[0:EP, :], away[0:EP, :], dst_f[0:EP, :], ALU.add) \
                    .then_inc(lead_ready, 1)

            def slot(r, k, part):
                m = k - L_FINAL
                if live(r, m):
                    dve.wait_ge(O_ready, tile(r, m + 1))
                    if isinstance(r, int) and r * RING + m >= MAIN + ORING:
                        dve.wait_ge(scattered, 16 * (r * RING + m - MAIN - ORING + 1))
                    elif live(r, m - ORING):
                        dve.wait_ge(stored[m % ORING // 2], (r * (RING // ORING) + m // ORING) * 16)
                    nc.vector.tensor_tensor(outs[:, m % ORING, :], O[:, :], rows[:, m % RING, :], ALU.add) \
                        .then_inc(final_ready, 1)
                if live(r, k + 1):
                    dve.wait_ge(yT_hi_ready, tile(r, k + 2))
                    if live(r, k - 1):
                        dve.wait_ge(U_ready, tile(r, k))
                    nc.vector.tensor_tensor(yT_lo[(k + 1) % 2][:, :], yT[:, :],
                                            yT_hi[(k + 1) % 2][:, :].bitcast(F32), ALU.subtract) \
                        .then_inc(yT_lo_ready, 1)
                if live(r, k - L_HT):
                    dve.wait_ge(hT_hi_ready, tile(r, k - L_HT + 1))
                    if live(r, k - L_HT - 2):
                        dve.wait_ge(O_ready, tile(r, k - L_HT - 1))
                    nc.vector.tensor_tensor(hT_lo[k % 2][:, :], HT[:, 0:HID], hT_hi[k % 2][:, :].bitcast(F32),
                                            ALU.subtract).then_inc(hT_lo_ready, 1)
                a = k - L_SCALE
                c = a % 4
                if k % 2 == 0 and live(r, a):
                    dve.wait_ge(tanh_ready, r * PAIRS + k // 2)
                    nc.vector.scalar_tensor_tensor(out=scale[:, c:c + 2, 0], in0=th[:, c:c + 2], scalar=1.0,
                                                   in1=half_rstd[:, c:c + 2], op0=ALU.add, op1=ALU.mult)
                    nc.vector.scalar_tensor_tensor(out=scale[:, c:c + 2, 1], in0=th[:, c:c + 2], scalar=1.0,
                                                   in1=half_rstd[:, c:c + 2], op0=ALU.subtract, op1=ALU.mult,
                                                   reverse0=True).then_inc(scale_ready, 1)
                t, j = sum_tile(r, k, part)
                if t is not None:
                    dve.wait_ge(C_free, t + 1)
                    nc.vector.tensor_copy(same_now[0:EP, :], same[0:EP, bass.ds(t, 1), :]
                                          .rearrange("p a e -> p (a e)")).then_inc(same_ready, 1)
                if k % 2 and live(r, k):
                    dve.wait_ge(U_ready, tile(r, k + 1))
                if live(r, a):
                    dve.wait_ge(scale_ready, r * PAIRS + k // 2)
                    if live(r, a - 2):
                        dve.wait_ge(hsum_ready, tile(r, a - 1))
                    for i in range(2):
                        last = nc.vector.scalar_tensor_tensor(out=hid[k % 2][:, i, :], in0=U[c][:, 0:HID],
                                                              scalar=scale[:, c, i:i + 1], in1=b1_bc[:, :],
                                                              op0=ALU.mult, op1=ALU.add)
                    last.then_inc(hid_in_ready, 1)
                if part in ("set0", "set1"):
                    if part == "set0" and k == FIRST:
                        dve.wait_ge(attr_loaded, 32)
                        dve.wait_ge(table_loaded, 32)
                        dve.wait_ge(x1_ready, ET)
                    paths = path_numbers(r, k, part)
                    segments = load_segments(mybir.EngineType.DVE, paths)
                    for (j, path, number), (i1, i2, _) in zip(paths, segments):
                        dve.wait_ge(prod_free, number + 1)
                        nc.vector.scalar_tensor_tensor(
                            out=prod[j % PB][0:EP, :, :], in0=x1[0:EP, set_tiles(part), bass.ds(i1, EXTENT)],
                            scalar=coef[0:EP, bass.ds(path, 1)], in1=x2[0:EP, set_tiles(part), bass.ds(i2, EXTENT)],
                            op0=ALU.mult, op1=ALU.mult).then_inc(multiplied, 1)
                if k % 2 and live(r, k):
                    pairs = r * PAIRS + (k + 1) // 2
                    c = (k - 1) % 4
                    nc.vector.max(top8[:, c, :], U[c][:, HID:WC])
                    nc.vector.max(top8[:, c + 1, :], U[c + 1][:, HID:WC]).then_inc(top_made, 1)
                    dve.wait_ge(top_made, pairs)
                    dve.wait_ge(rstd_ready, pairs)
                    for i in (c, c + 1):
                        last = nc.vector.scalar_tensor_tensor(out=half_gap[:, i:i + 1], in0=top8[:, i, 0:1],
                                                              scalar=top8[:, i, 1:2], in1=half_rstd[:, i:i + 1],
                                                              op0=ALU.subtract, op1=ALU.mult)
                    last.then_inc(half_gap_ready, 1)
                if isinstance(r, int) and r == 0 and FIRST <= k < FIRST + ET // SRC_PER:
                    t = SRC_PER * (k - FIRST)
                    for i in range(SETS):
                        dve.wait_ge(x1_loaded[i], 16 * SET)
                    for i in range(SRC_PER):
                        last = nc.vector.bn_stats(src_stats[0:EP, t + i, :], x1[0:EP, t + i, :])
                    last.then_inc(src_stats_made, 1)
                    dve.wait_ge(src_stats_made, k - FIRST + 1)
                    for i in range(SRC_PER):
                        last = nc.vector.bn_aggr(src_mv[0:EP, t + i, :], src_stats[0:EP, t + i, :])
                    last.then_inc(src_var_ready, 1)
                if isinstance(r, int) and r == 0 and k == FIRST + ET // SRC_PER:
                    dve.wait_ge(src_rstd_ready, 1)
                    nc.vector.scalar_tensor_tensor(out=src_shift[0:EP, :], in0=src_mv[0:EP, :, 0], scalar=-1.0,
                                                   in1=src_rstd[0:EP, :], op0=ALU.mult, op1=ALU.mult) \
                        .then_inc(src_shift_ready, 1)
                if isinstance(r, int) and r == 0 and FIRST + ET // SRC_PER <= k < FIRST + 2 * ET // SRC_PER:
                    for i in range(SRC_PER):
                        repeats_of(SRC_PER * (k - FIRST) - ET + i)
                    if k == FIRST + 2 * ET // SRC_PER - 1:
                        leaders()

            rounds(dve, slot)

        @block.gpsimd
        def _(pool):
            nc.gpsimd.memset(mean_mat, 1.0 / D).then_inc(pool_const, 1)
            nc.gpsimd.memset(twos, 2.0)
            nc.gpsimd.memset(ident[:, :], 0.0)
            nc.gpsimd.memset(later, 0.0).then_inc(pool_const, 1)
            pool.wait_ge(pool_const, 2)
            nc.gpsimd.affine_select(out=ident[:, :], in_=ident[:, :], compare_op=ALU.not_equal, fill=1.0,
                                    base=0, pattern=[[-1, P]], channel_multiplier=1).then_inc(pool_const, 1)
            nc.gpsimd.affine_select(out=later, in_=later, compare_op=ALU.is_ge, fill=1.0,
                                    base=0, pattern=[[-1, P]], channel_multiplier=1)
            nc.gpsimd.iota(spare_i[:, :], pattern=[[0, 1]], base=N, channel_multiplier=1).then_inc(pool_const, 1)
            nc.gpsimd.memset(minus_half[:, :], -0.5)
            nc.gpsimd.memset(ones[:, :].bitcast(F32), 1.0)
            nc.gpsimd.memset(bias_rows[:, :].bitcast(F32), 0.0).then_inc(bias_zero, 1)

            pool.wait_ge(index_loaded, 32)
            for t in range(ET):
                nc.gpsimd.indirect_dma_start(
                    out=x1[0:EP, t, :], out_offset=None, in_=x,
                    in_offset=bass.IndirectOffsetOnAxis(ap=src_i[0:EP, t:t + 1], axis=0),
                ).then_inc(x1_loaded[t // SET], 16)
            pool.dma_start(y_rows[N:N + P, :], x[0:P, :]).then_inc(summed, 16)

            def slot(r, k, part):
                s = k - FIRST
                if isinstance(r, int) and r == 0 and s == 0:
                    nc.gpsimd.memset(acc[0:EP, dst_tiles:SET, :], 0.0)
                if isinstance(r, int) and r == 0 and s == 3:
                    nc.gpsimd.memset(acc[0:EP, SET:ET - 3, :], 0.0)
                if isinstance(r, int) and r == 0 and s == 6:
                    nc.gpsimd.memset(acc[0:EP, ET - 3:ET, :], 0.0)
                if isinstance(r, int) and r == 0 and s == RING - 1:
                    pool.wait_ge(eq_made, 2 * ET)
                    nc.gpsimd.memset(acc[0:EP, 0:dst_tiles, :], 0.0).then_inc(prod_free, PB)

                if part in ("set0", "set1") and k > FIRST:
                    if part == "set0" and k == FIRST + 1:
                        pool.wait_ge(table_loaded, 32)
                    paths = path_numbers(r, k - 1, part)
                    segments = load_segments(mybir.EngineType.Pool, paths)
                    for (j, path, number), (_, _, i3) in zip(paths, segments):
                        pool.wait_ge(multiplied, number + 1)
                        pool.wait_ge(prod_free, number + PB)
                        sums = acc[0:EP, set_tiles(part), bass.ds(i3, EXTENT)]
                        nc.gpsimd.tensor_tensor(sums, sums, prod[j % PB][0:EP, :, :], ALU.add).then_inc(prod_free, 1)

                t0, j0 = sum_tile(r, k - 2, part) if s >= 2 else (None, None)
                if t0 is not None:
                    pool.wait_ge(summed, t0 * 16 + 16)
                    pool.wait_ge(C_free, t0 + 2)
                if part == "set1" and s == 0:
                    pool.wait_ge(y_filled, 16 * FILLS)
                    pool.wait_ge(summed, (r - SET1[0]) * (SET // 2) * 16 + 16)
                if part == "set1" and s == 1:
                    pool.wait_ge(index_copied, r - SET1[0] + 1)
                if k % 2 and live(r, k):
                    pool.wait_ge(squares_ready, tile(r, k + 1))
                    if live(r, k - 4):
                        pool.wait_ge(scale_ready, r * PAIRS + k // 2 - 1)
                a = k - L_SUM
                if live(r, a):
                    pool.wait_ge(hid_ready, tile(r, a + 1))
                    if live(r, a - 2):
                        pool.wait_ge(HT_ready, tile(r, a - 1))
                    nc.gpsimd.tensor_tensor(hsum[a % 2][:, :], hid[a % 2][:, 0, :], hid[a % 2][:, 1, :], ALU.add) \
                        .then_inc(hsum_ready, 1)
                if part == "set1" and s == 0:
                    pool.wait_ge(lead_ready, 1)
                    t = (r - SET1[0]) * (SET // 2)
                    nc.gpsimd.tensor_copy(put_i[0:EP, :], lead_i[0:EP, bass.ds(t, SET // 2)]) \
                        .then_inc(index_copied, 1)
                if k % 2 and live(r, k):
                    c = (k - 1) % 4
                    nc.gpsimd.tensor_scalar(var4[:, c:c + 2], squares[:, c:c + 2], 4.0 / D, 4.0 * EPS,
                                            ALU.mult, ALU.add).then_inc(var4_made, 1)
                    pool.wait_ge(var4_made, r * PAIRS + k // 2 + 1)
                    nc.gpsimd.tensor_tensor(half_rstd[:, c:c + 2], var4[:, c:c + 2], minus_half[:, 0:2],
                                            ALU.pow).then_inc(rstd_ready, 1)

                if isinstance(r, int) and r == 0 and k == FIRST + ET // SRC_PER - 1:
                    pool.wait_ge(src_var_ready, ET // SRC_PER)
                    nc.gpsimd.tensor_scalar(src_rstd[0:EP, :], src_mv[0:EP, :, 1], EPS, 1.0,
                                            ALU.add, ALU.mult).then_inc(src_rstd_step, 1)
                    pool.wait_ge(src_rstd_step, 1)
                    nc.gpsimd.tensor_tensor(src_rstd[0:EP, :], src_rstd[0:EP, :], minus_half[0:EP, :],
                                            ALU.pow).then_inc(src_rstd_ready, 1)
                if t0 is not None:
                    where = put_i[0:EP, s // 2 - 1:s // 2] if part == "set1" else lead_i[0:EP, t0:t0 + 1]
                    nc.gpsimd.indirect_dma_start(
                        out=y_rows, out_offset=bass.IndirectOffsetOnAxis(ap=where, axis=0),
                        in_=moved[j0][0:EP, :], in_offset=None, compute_op=ALU.add).then_inc(summed, 16)
                if isinstance(r, int) and MAIN <= r * RING + k + L_GATHER < TILES:
                    m = r * RING + k + L_GATHER
                    if m == MAIN:
                        pool.wait_ge(summed, 16 * ET + 16)
                    pool.wait_ge(final_ready, m - RING + 1)
                    nc.gpsimd.indirect_dma_start(
                        out=rows[0:EP, m % RING, :], out_offset=None, in_=y_rows,
                        in_offset=bass.IndirectOffsetOnAxis(ap=dst_i[0:EP, m - MAIN:m - MAIN + 1], axis=0),
                    ).then_inc(edge_loaded[m % RING], 16)
                if isinstance(r, int) and MAIN <= r * RING + k - L_STORE < TILES:
                    m = r * RING + k - L_STORE
                    if m == MAIN:
                        for i in range(2):
                            pool.wait_ge(stored[i], 16 * (MAIN_PAIRS // 2))
                    pool.wait_ge(final_ready, m + 1)
                    if m > MAIN:
                        pool.wait_ge(scattered, 16 * (m - MAIN))
                    nc.gpsimd.indirect_dma_start(
                        out=out, out_offset=bass.IndirectOffsetOnAxis(ap=lead_i[0:EP, m - MAIN:m - MAIN + 1], axis=0),
                        in_=outs[0:EP, m % ORING, :], in_offset=None,
                        bounds_check=N - 1, oob_is_err=False).then_inc(scattered, 16)

            rounds(pool, slot)
            pool.wait_ge(scattered, 16 * ET)

        @block.tensor
        def _(pe):
            pe.wait_ge(pool_const, 4)
            pe.wait_ge(w_loaded, 16 * (DC + 1))
            for c in range(DC):
                last = nc.tensor.matmul(U[0][:, 0:WC], mean_mat, w_raw[:, c, :], start=(c == 0), stop=(c == DC - 1))
            last.then_inc(col_mean, 1)
            pe.wait_ge(bias_loaded, 32)
            nc.tensor.matmul(C[:, :], twos[0:EXPERTS, :], b2_raw, start=True, stop=True).then_inc(bias_sum, 1)

            def slot(r, k, part):
                if live(r, k + 1):
                    wait_rows(pe, r, k + 1)
                    if live(r, k):
                        pe.wait_ge(yT_lo_ready, tile(r, k + 1))
                    for c in range(DC):
                        last = nc.tensor.transpose(yT[:, c * P:(c + 1) * P],
                                                   rows[:, (k + 1) % RING, c * P:(c + 1) * P], ident[:, :])
                    last.then_inc(yT_ready, 1)
                m = k - L_HT
                if live(r, m):
                    pe.wait_ge(hsum_ready, tile(r, m + 1))
                    if live(r, m - 1):
                        pe.wait_ge(hT_lo_ready, tile(r, m))
                    for h in range(HC):
                        last = nc.tensor.transpose(HT[:, h * P:(h + 1) * P], hsum[m % 2][:, h * P:(h + 1) * P],
                                                   ident[:, :])
                    last.then_inc(HT_ready, 1)
                if live(r, k):
                    if isinstance(r, int) and r == 0 and k == 0:
                        pe.wait_ge(w_ready, 1)
                        pe.wait_ge(yT_lo_ready, 1)
                    if not live(r, k + 1):
                        pe.wait_ge(yT_lo_ready, tile(r, k + 1))
                    if live(r, k - 4):
                        pe.wait_ge(hid_in_ready, tile(r, k - 3))
                    u = U[k % 4][:, 0:WC]
                    hi, lo = yT_hi[k % 2], yT_lo[k % 2]
                    for c in range(DC):
                        cc = slice(c * P, (c + 1) * P)
                        nc.tensor.matmul(u, hi[:, cc], w_hi[:, c, :], start=(c == 0), stop=False)
                        nc.tensor.matmul(u, hi[:, cc], w_lo[:, c, :], start=False, stop=False)
                        last = nc.tensor.matmul(u, lo[:, cc], w_hi[:, c, :], start=False, stop=(c == DC - 1))
                    last.then_inc(U_ready, 1)
                m = k - L_DOWN
                if live(r, m):
                    if isinstance(r, int) and r * RING + m == 0:
                        pe.wait_ge(bias_moved, 16)
                        pe.wait_ge(w_ready, 2)
                    if live(r, m - 1):
                        pe.wait_ge(final_ready, tile(r, m))
                    nc.tensor.matmul(O[:, :], ones[:, :], bias_rows[:, :], start=True, stop=False)
                    pe.wait_ge(hT_lo_ready, tile(r, m + 1))
                    hi, lo = hT_hi[m % 2], hT_lo[m % 2]
                    for h in range(HC):
                        hh = slice(h * P, (h + 1) * P)
                        nc.tensor.matmul(O[:, :], hi[:, hh], w2_hi[:, h, :], start=False, stop=False)
                        nc.tensor.matmul(O[:, :], hi[:, hh], w2_lo[:, h, :], start=False, stop=False)
                        last = nc.tensor.matmul(O[:, :], lo[:, hh], w2_hi[:, h, :], start=False, stop=(h == HC - 1))
                    last.then_inc(O_ready, 1)
                t, j = sum_tile(r, k, part)
                if t is not None:
                    if k == FIRST:
                        pe.wait_ge(prod_free, PB + (NP if part == "set1" else 2 * NP))
                    pe.wait_ge(same_ready, t + 1)
                    pe.wait_ge(C_free, t + 1)
                    nc.tensor.matmul(C[0:EP, :], same_now[0:EP, :],
                                     acc[0:EP, bass.ds(t, 1), :].rearrange("p a d -> p (a d)"),
                                     start=True, stop=True).then_inc(comb_ready, 1)

            rounds(pe, slot)


_INS = ["x", "src", "dst", "edge_attr_512", "L0_gnn_path_coeffs", "L0_gnn_path_indices",
        "L0_ffn_Wg", "L0_ffn_W1", "L0_ffn_b1", "L0_ffn_W2", "L0_ffn_b2"]


def kernel(**inputs):
    import numpy as _np
    import concourse.bacc as _bacc
    from concourse import mybir as _mybir
    from concourse.bass_utils import run_bass_kernel_spmd as _run

    nc = _bacc.Bacc("TRN2", target_bir_lowering=False, num_devices=1)
    arrays, args = {}, []
    for name in _INS:
        a = _np.ascontiguousarray(inputs[name])
        arrays[f"in_{name}"] = a
        args.append(nc.dram_tensor(f"in_{name}", a.shape, _mybir.dt.from_np(a.dtype), kind="ExternalInput").ap())
    shape = inputs["x"].shape
    args.append(nc.dram_tensor("out_rows", shape, _mybir.dt.float32, kind="ExternalOutput").ap())
    gnn_ffn_kernel(nc, *args)
    r = _run(nc, [arrays], core_ids=[0])
    return r.results[0]["out_rows"]
```

```python
import numpy as np
import concourse.bass as bass
from concourse import mybir
from contextlib import ExitStack


def gnn_ffn_kernel(nc, x, src, dst, edge_attr, path_coeffs, path_indices, Wg, W1, b1, W2, b2, out):
    F32 = mybir.dt.float32
    F32R = mybir.dt.float32r
    BF16 = mybir.dt.bfloat16
    U8 = mybir.dt.uint8
    I32 = mybir.dt.int32
    ALU = mybir.AluOpType
    ACT = mybir.ActivationFunctionType

    N, D = x.shape
    NE = src.shape[0]
    NP = path_coeffs.shape[0]
    EXPERTS, _, DFF = W1.shape
    HID = EXPERTS * DFF
    WC = HID + EXPERTS
    EXTENT = 32
    NSEG = D // EXTENT
    EPS = 1e-5
    P = 128
    DC = D // P
    HC = HID // P

    ET = 20
    EP = NE // ET
    assert EP * ET == NE and EP <= P
    SET = ET // 2
    SETS = 2

    RING = 12
    PAIRS = RING // 2
    ORING = 4
    FIRST = 4
    MAIN_PAIRS = -(-N // (2 * P))
    MAIN = 2 * MAIN_PAIRS
    TILES = MAIN + ET
    ROUNDS = (TILES - FIRST) // RING
    assert FIRST + ROUNDS * RING == TILES and MAIN % ORING == 0
    L_SCALE, L_SUM, L_HT, L_DOWN, L_FINAL, L_STORE, L_GATHER = 2, 3, 4, 4, 5, 6, 4
    SET0, SET1, SUM1 = (1, 3), (3, 5), 5
    LESS_SLOTS = 7
    PPR = NP // 2
    PER_SLOT = [3] * 10 + [2, 0]
    PB = 4
    DST_GROUP, GROUP = 4, 3
    ATTR_SLOTS = (6, 9)
    CLEAR_SLOT = 6
    DST_SLOT, STATS_SLOT = -1, 6
    NORM_SLOT = STATS_SLOT + 3
    FETCH_FIRST, FETCH = 12, 2
    FILLS_LOOPED = 10
    FILLS = RING + FILLS_LOOPED * (SET0[1] - SET0[0])
    FILL = N * D // FILLS
    assert FILL * FILLS == N * D and FILL % 16 == 0
    assert sum(PER_SLOT) == PPR and len(PER_SLOT) == RING

    y_rows = nc.dram_tensor("y_rows", (N + P, D), F32, kind="Internal").ap()
    y_flat = y_rows.rearrange("n d -> (n d)")
    x_flat = x.rearrange("n d -> (n d)")

    def pair_rows(dram, q):
        base = q * 2 * P
        if isinstance(q, int):
            base = min(base, N - 2 * P)
        return dram[bass.ds(base, 2 * P), :].rearrange("(p j) d -> p j d", j=2)

    ctx = ExitStack()
    with ctx:
        def sb(name, shape, dt=F32):
            return ctx.enter_context(nc.sbuf_tensor(name, shape, dt))

        def pb(name, shape):
            return ctx.enter_context(nc.psum_tensor(name, shape, F32))

        def sem(name):
            return ctx.enter_context(nc.semaphore(name))

        rows = sb("rows", [P, RING, D])
        outs = sb("outs", [P, ORING, D])
        x1 = sb("x1", [P, ET, D])
        x2 = sb("x2", [P, ET, D])
        acc = sb("acc", [P, ET, D])
        same = sb("same", [P, ET, EP], U8)
        same_now = sb("same_now", [P, EP])
        prod = [sb(f"prod{i}", [P, SET, EXTENT]) for i in range(PB)]
        yT_hi = [sb(f"yT_hi{i}", [P, D], F32R) for i in range(2)]
        yT_lo = [sb(f"yT_lo{i}", [P, D], F32R) for i in range(2)]
        w_hi = sb("w_hi", [P, DC, WC], F32R)
        w_lo = sb("w_lo", [P, DC, WC], F32R)
        w2_hi = sb("w2_hi", [P, HC, D], F32R)
        w2_lo = sb("w2_lo", [P, HC, D], F32R)
        hid = [sb(f"hid{i}", [P, 2, HID]) for i in range(2)]
        hsum = [sb(f"hsum{i}", [P, HID]) for i in range(2)]
        hT_hi = [sb(f"hT_hi{i}", [P, HID], F32R) for i in range(2)]
        hT_lo = [sb(f"hT_lo{i}", [P, HID], F32R) for i in range(2)]
        moved = [sb(f"moved{i}", [P, D]) for i in range(2)]
        b1_bc = sb("b1_bc", [P, HID])
        bias_rows = sb("bias_rows", [P, D], F32R)
        ones = sb("ones", [P, P], F32R)
        ident = sb("ident", [P, P])
        minus_ident = sb("minus_ident", [P, P], F32R)
        coef = sb("coef", [P, NP])
        table = sb("table", [1, NP * 3], I32)
        src_i = sb("src_i", [P, ET], I32)
        dst_i = sb("dst_i", [P, ET], I32)
        dst_f = sb("dst_f", [P, ET])
        repeats = sb("repeats", [P, ET])
        away = sb("away", [P, ET])
        lead_i = sb("lead_i", [P, ET], I32)
        spare_i = sb("spare_i", [P, 1], I32)
        spare_f = sb("spare_f", [P, 1])
        put_i = sb("put_i", [P, SET // 2], I32)
        src_stats = sb("src_stats", [P, ET, 6])
        src_mv = sb("src_mv", [P, ET, 2])
        src_rstd = sb("src_rstd", [P, ET])
        src_shift = sb("src_shift", [P, ET])
        unused = sb("unused", [P, D], BF16)
        minus_mean = sb("minus_mean", [P, 4])
        squares = sb("squares", [P, 4])
        var4 = sb("var4", [P, 4])
        half_rstd = sb("half_rstd", [P, 4])
        minus_half = sb("minus_half", [P, GROUP])
        top8 = sb("top8", [P, 4, 8])
        half_gap = sb("half_gap", [P, 4])
        th = sb("th", [P, 4])
        scale = sb("scale", [P, 4, 2])

        yT = [pb(f"yT{i}", [P, D]) for i in range(2)]
        U = [pb(f"U{i}", [P, 512]) for i in range(3)]
        HT = pb("HT", [P, 512])
        O = pb("O", [P, D])
        C = pb("C", [P, D])

        w_raw = outs[:, :, :].rearrange("p a d -> p (a d)")[:, 0:DC * WC].rearrange("p (c n) -> p c n", c=DC)
        w2_raw = [hid[h][:, :, :].rearrange("p a f -> p (a f)") for h in range(HC)]
        b2_raw = moved[0][0:EXPERTS, :]
        LO = 32
        bias_hi = moved[1][LO:LO + 1, :].bitcast(F32R)
        mean_mat = prod[0][:, :, :].rearrange("p t u -> p (t u)")[:, 0:P]
        twos = prod[1][:, :, :].rearrange("p t u -> p (t u)")[:, 0:P]
        all_dst = acc[:, :, :].rearrange("p t d -> p (t d)")[:, 0:NE].bitcast(I32) \
            .rearrange("p (e t) -> p e t", t=ET)
        dst_tiles = -(-NE // D)
        table_raw = prod[0][:, :, :].rearrange("p t u -> p (t u)")[0:1, P:P + 3 * NP].bitcast(I32)
        later = prod[3][:, :, :].rearrange("p t u -> p (t u)")[:, 0:P]
        scratch = prod[2][:, :, :].rearrange("p t u -> p (t u)")[0:EP, 0:EP]

        x_loaded = [sem(f"x_loaded{i}") for i in range(PAIRS)]
        edge_loaded = [sem(f"edge_loaded{i}") for i in range(RING)]
        w_loaded = sem("w_loaded")
        w2_loaded = sem("w2_loaded")
        bias_loaded = sem("bias_loaded")
        index_loaded = sem("index_loaded")
        all_dst_loaded = sem("all_dst_loaded")
        table_loaded = sem("table_loaded")
        table_ready = sem("table_ready")
        attr_loaded = sem("attr_loaded")
        x1_loaded = [sem(f"x1_loaded{i}") for i in range(SETS)]
        pool_const = sem("pool_const")
        col_mean = sem("col_mean")
        w_centered = sem("w_centered")
        w_rounded = sem("w_rounded")
        w_ready = sem("w_ready")
        bias_sum = sem("bias_sum")
        bias_hi_made = sem("bias_hi_made")
        bias_zero = sem("bias_zero")
        src_stats_made = sem("src_stats_made")
        src_var_ready = sem("src_var_ready")
        src_rstd_step = sem("src_rstd_step")
        src_rstd_ready = sem("src_rstd_ready")
        src_shift_ready = sem("src_shift_ready")
        x1_ready = sem("x1_ready")
        dst_made = sem("dst_made")
        eq_made = sem("eq_made")
        lead_step = sem("lead_step")
        lead_ready = sem("lead_ready")
        multiplied = sem("multiplied")
        prod_free = sem("prod_free")
        index_copied = sem("index_copied")
        y_filled = sem("y_filled")
        same_ready = sem("same_ready")
        comb_ready = sem("comb_ready")
        C_free = sem("C_free")
        summed = sem("summed")
        yT_ready = sem("yT_ready")
        yT_hi_ready = sem("yT_hi_ready")
        yT_lo_ready = sem("yT_lo_ready")
        yT_less_ready = sem("yT_less_ready")
        U_ready = sem("U_ready")
        mean_made = sem("mean_made")
        squares_ready = sem("squares_ready")
        var4_made = sem("var4_made")
        rstd_ready = sem("rstd_ready")
        top_made = sem("top_made")
        half_gap_ready = sem("half_gap_ready")
        tanh_ready = sem("tanh_ready")
        scale_ready = sem("scale_ready")
        hid_in_ready = sem("hid_in_ready")
        hid_ready = sem("hid_ready")
        hsum_ready = sem("hsum_ready")
        HT_ready = sem("HT_ready")
        hT_hi_ready = sem("hT_hi_ready")
        hT_lo_ready = sem("hT_lo_ready")
        O_ready = sem("O_ready")
        final_ready = sem("final_ready")
        stored = [sem(f"stored{i}") for i in range(ORING // 2)]
        scattered = sem("scattered")

        block = ctx.enter_context(nc.Block())

        def rounds(eng, slot):
            for k in range(-1, FIRST):
                slot(0, k, None)
            for k in range(FIRST, FIRST + RING):
                slot(0, k, None)
            for part, (r0, r1) in (("set0", SET0), ("set1", SET1)):
                with eng.Fori(r0, r1) as r:
                    for k in range(FIRST, FIRST + RING):
                        slot(r, k, part)
            for r in range(SUM1, ROUNDS):
                for k in range(FIRST, FIRST + RING):
                    slot(r, k, "sum1" if r == SUM1 else None)
            for k in range(FIRST, FIRST + L_STORE + 1):
                slot(ROUNDS, k, None)

        def live(r, k):
            return 0 <= r * RING + k < TILES if isinstance(r, int) else True

        def tile(r, k):
            return r * RING + k

        def without_vector(r, k, part):
            return part in ("set0", "set1") or isinstance(r, int) and r == 0 and FIRST <= k < FIRST + LESS_SLOTS

        def less_count(r, k, part):
            return k - FIRST + 1 + (0 if part is None else LESS_SLOTS + (r - SET0[0]) * RING)

        def is_edge(r, k):
            return isinstance(r, int) and r * RING + k >= MAIN

        def wait_rows(eng, r, k):
            if is_edge(r, k):
                eng.wait_ge(edge_loaded[k % RING], 16 * ((r * RING + k - MAIN) // RING + 1))
            else:
                eng.wait_ge(x_loaded[k % RING // 2], (r + k // RING) * 16 + 16)

        def source_tiles(r, g):
            return range(GROUP * g, min(GROUP * g + GROUP, ET)) if isinstance(r, int) and r == 0 and g >= 0 else ()

        def slot_paths(k):
            first = sum(PER_SLOT[:k - FIRST])
            return range(first, first + PER_SLOT[k - FIRST])

        def set_tiles(part):
            return slice(0, SET) if part == "set0" else slice(SET, ET)

        def path_numbers(r, k, part):
            first = (r - (SET0 if part == "set0" else SET1)[0]) * PPR
            return [(j, first + j, (r - SET0[0]) * PPR + j) for j in slot_paths(k)]

        segments = {}

        def load_segments(engine, r, k, part):
            if (k - FIRST) % 2 == 0:
                paths = path_numbers(r, k, part) + path_numbers(r, k + 1, part)
                first, width = (paths[0][1] * 2, 2) if engine == mybir.EngineType.DVE else (2 * NP + paths[0][1], 1)
                _, values = nc.values_load_multi_w_load_instructions(
                    table[0:1, bass.ds(first, width * len(paths))], engines=(engine,), min_val=0, max_val=NSEG - 1,
                    skip_runtime_bounds_check_because="the segment numbers of a path are below NSEG")
                for i, (_, path, _) in enumerate(paths):
                    segments[engine, paths[i][0]] = [v * EXTENT for v in values[i * width:(i + 1) * width]]
            return [(j, path, number, segments[engine, j]) for j, path, number in path_numbers(r, k, part)]

        def sum_tile(r, k, part):
            s = k - FIRST
            if part == "set1" and s % 2 == 0 and s // 2 < SET // 2:
                return (r - SET1[0]) * (SET // 2) + s // 2, s // 2 % 2
            if part == "sum1" and 0 <= s < SET:
                return SET + s, s % 2
            return None, None

        @block.sync
        def _(sp):
            def load(q, i):
                sp.dma_start(rows[:, 2 * i:2 * i + 2, :], pair_rows(x, q)).then_inc(x_loaded[i], 16)

            def store(q, i):
                sp.dma_start(pair_rows(out, q), outs[:, 2 * (i % 2):2 * (i % 2) + 2, :]) \
                    .then_inc(stored[i % 2], 16)

            for c in range(DC):
                sp.dma_start(w_raw[:, c, 0:HID].rearrange("p (e f) -> p e f", e=EXPERTS),
                             W1[:, c * P:(c + 1) * P, :].rearrange("e p f -> p e f")).then_inc(w_loaded, 16)
            sp.dma_start(w_raw[:, :, HID:WC], Wg.rearrange("(c p) e -> p c e", p=P)).then_inc(w_loaded, 16)
            load(0, 0)
            sp.dma_start(all_dst[0:EP, :, :], dst.rearrange("(p t) -> p t", t=ET).partition_broadcast(EP)) \
                .then_inc(all_dst_loaded, 16)
            for q in range(1, PAIRS):
                load(q, q)
            sp.dma_start(table_raw, path_indices.rearrange("n c -> (n c)").unsqueeze(0)).then_inc(table_loaded, 16)
            sp.dma_start(coef[:, :], path_coeffs.partition_broadcast(P)).then_inc(table_loaded, 16)
            loops = (MAIN_PAIRS - PAIRS) // PAIRS
            with sp.Fori(0, loops) as r:
                for i in range(PAIRS):
                    q = r * PAIRS + i
                    sp.wait_ge(final_ready, q * 2 + 2)
                    store(q, i)
                    load(q + PAIRS, i)
            for q in range(loops * PAIRS, MAIN_PAIRS):
                sp.wait_ge(final_ready, 2 * q + 2)
                if q == MAIN_PAIRS - 1:
                    sp.wait_ge(stored[(q - 1) % 2], 16 * ((q - 1) // 2 + 1))
                store(q, q % PAIRS)
                if q + PAIRS < MAIN_PAIRS:
                    load(q + PAIRS, q % PAIRS)
            for i in range(2):
                sp.wait_ge(stored[i], 16 * (MAIN_PAIRS // 2))

        @block.scalar
        def _(act):
            act.dma_start(src_i[0:EP, :], src.rearrange("(p t) -> p t", t=ET)).then_inc(index_loaded, 16)
            act.dma_start(dst_i[0:EP, :], dst.rearrange("(p t) -> p t", t=ET)).then_inc(index_loaded, 16)
            act.dma_start(b2_raw, b2).then_inc(bias_loaded, 16)
            act.dma_start(b1_bc[:, :], b1.rearrange("e f -> (e f)").partition_broadcast(P)).then_inc(bias_loaded, 16)
            for h in range(HC):
                act.dma_start(w2_raw[h], W2.rearrange("e f d -> (e f) d")[h * P:(h + 1) * P, :]) \
                    .then_inc(w2_loaded, 16)
            act.wait_ge(pool_const, 3)
            nc.scalar.activation(minus_ident[:, :], ident[:, :], ACT.Copy, scale=-1.0)
            act.wait_ge(w_centered, 1)
            nc.scalar.activation(w_hi[:, :, :], w_raw, ACT.Copy).then_inc(w_rounded, 1)

            def slot(r, k, part):
                s = k - FIRST
                if part == "set0" and s < FILLS_LOOPED or isinstance(r, int) and r == 0 and 0 <= s < RING:
                    f = s if part is None else RING + (r - SET0[0]) * FILLS_LOOPED + s
                    act.dma_start(y_flat[bass.ds(f * FILL, FILL)].rearrange("(a r) -> a r", a=16),
                                  x_flat[bass.ds(f * FILL, FILL)].rearrange("(a r) -> a r", a=16)) \
                        .then_inc(y_filled, 16)
                if live(r, k - L_HT):
                    act.wait_ge(HT_ready, tile(r, k - L_HT + 1))
                    if live(r, k - L_HT - 2):
                        act.wait_ge(O_ready, tile(r, k - L_HT - 1))
                    nc.scalar.activation(hT_hi[k % 2][:, :], HT[:, 0:HID], ACT.Copy).then_inc(hT_hi_ready, 1)
                if isinstance(r, int) and r == 0 and k in ATTR_SLOTS:
                    tt = slice(SET * ATTR_SLOTS.index(k), SET * ATTR_SLOTS.index(k) + SET)
                    attr = edge_attr.rearrange("(p t) d -> p t d", t=ET)
                    even = EP // 8 * 8
                    for lo, hi in ((0, even), (even, EP)):
                        act.dma_start(x2[lo:hi, tt, :].rearrange("p t d -> p (t d)"),
                                      attr[lo:hi, tt, :].rearrange("p t d -> p (t d)")).then_inc(attr_loaded, 16)
                if live(r, k + 1):
                    act.wait_ge(yT_ready, tile(r, k + 2))
                    if live(r, k - 1):
                        act.wait_ge(U_ready, tile(r, k))
                    nc.scalar.activation(yT_hi[(k + 1) % 2][:, :], yT[(k + 1) % 2][:, :], ACT.Copy) \
                        .then_inc(yT_hi_ready, 1)
                if k % 2 == 0 and live(r, k - 2):
                    act.wait_ge(half_gap_ready, r * PAIRS + k // 2)
                    c = (k - 2) % 4
                    nc.scalar.activation(th[:, c:c + 2], half_gap[:, c:c + 2], ACT.Tanh).then_inc(tanh_ready, 1)
                if live(r, k + 1):
                    c = (k + 1) % 4
                    wait_rows(act, r, k + 1)
                    if live(r, k):
                        act.wait_ge(squares_ready, tile(r, k + 1))
                    nc.scalar.activation(unused[:, :], rows[:, (k + 1) % RING, :], ACT.Copy, scale=-1.0 / D,
                                         accum_out=minus_mean[:, c:c + 1]).then_inc(mean_made, 1)
                if isinstance(r, int) and r == 0 and k == 0:
                    act.wait_ge(w2_loaded, 16 * HC)
                    for h in range(HC):
                        last = nc.scalar.activation(w2_hi[:, h, :], w2_raw[h], ACT.Copy)
                    last.then_inc(w_rounded, 1)
                    act.wait_ge(bias_sum, 1)
                    act.wait_ge(bias_zero, 1)
                    nc.scalar.activation(bias_rows[0:1, :], C[0:1, :], ACT.Copy)
                    nc.scalar.activation(bias_hi, C[LO:LO + 1, :], ACT.Copy).then_inc(bias_hi_made, 1)
                t, j = sum_tile(r, k - 1, part)
                if t is not None:
                    act.wait_ge(comb_ready, t + 1)
                    if part == "set1" or t == SET:
                        act.wait_ge(summed, t * 16 + 16)
                    else:
                        act.wait_ge(summed, t * 16)
                    nc.scalar.activation(moved[j][0:EP, :], C[0:EP, :], ACT.Copy).then_inc(C_free, 1)
                if live(r, k + 1):
                    c = (k + 1) % 4
                    act.wait_ge(mean_made, tile(r, k + 2))
                    if live(r, k - 3):
                        act.wait_ge(var4_made, r * PAIRS + (k - 1) // 2)
                    nc.scalar.activation(unused[:, :], rows[:, (k + 1) % RING, :], ACT.Square,
                                         bias=minus_mean[:, c:c + 1],
                                         accum_out=squares[:, c:c + 1]).then_inc(squares_ready, 1)
                if live(r, k + 1) and without_vector(r, k, part):
                    act.wait_ge(yT_less_ready, less_count(r, k, part))
                    if live(r, k - 1):
                        act.wait_ge(U_ready, tile(r, k))
                    nc.scalar.activation(yT_lo[(k + 1) % 2][:, :], yT[(k + 1) % 2][:, :], ACT.Copy) \
                        .then_inc(yT_lo_ready, 1)
                tiles = source_tiles(r, k - NORM_SLOT)
                for t in tiles[:2]:
                    act.wait_ge(src_shift_ready, k - NORM_SLOT + 1)
                    nc.scalar.activation(x1[0:EP, t, :], x1[0:EP, t, :], ACT.Identity,
                                         scale=src_rstd[0:EP, t:t + 1], bias=src_shift[0:EP, t:t + 1]) \
                        .then_inc(x1_ready, 1)
                if live(r, k - L_SCALE):
                    act.wait_ge(hid_in_ready, tile(r, k - L_SCALE + 1))
                    nc.scalar.activation(hid[k % 2][:, :, :], hid[k % 2][:, :, :], ACT.Gelu).then_inc(hid_ready, 1)

            rounds(act, slot)

        @block.vector
        def _(dve):
            dve.wait_ge(col_mean, 1)
            for c in range(DC):
                last = nc.vector.tensor_tensor(w_raw[:, c, :], w_raw[:, c, :], U[0][:, 0:WC], ALU.subtract)
            last.then_inc(w_centered, 1)
            dve.wait_ge(w_rounded, 1)
            nc.vector.tensor_tensor(w_lo[:, :, :], w_raw, w_hi[:, :, :].bitcast(F32), ALU.subtract).then_inc(w_ready, 1)

            def repeats_of(t):
                if t == 0:
                    dve.wait_ge(index_loaded, 32)
                    dve.wait_ge(all_dst_loaded, 16)
                    dve.wait_ge(pool_const, 4)
                    nc.vector.tensor_copy(dst_f[0:EP, :], dst_i[0:EP, :]).then_inc(dst_made, 1)
                    nc.vector.tensor_copy(spare_f[:, :], spare_i[:, :]).then_inc(dst_made, 1)
                    dve.wait_ge(dst_made, 2)
                nc.vector.tensor_scalar(same[0:EP, t, :], all_dst[0:EP, :, t], dst_f[0:EP, t:t + 1], None,
                                        ALU.is_equal).then_inc(eq_made, 1)
                dve.wait_ge(eq_made, 2 * t + 1)
                nc.vector.scalar_tensor_tensor(out=scratch, in0=same[0:EP, t, :], scalar=1.0,
                                               in1=later[0:EP, 0:EP], op0=ALU.mult, op1=ALU.mult,
                                               accum_out=repeats[0:EP, t:t + 1]).then_inc(eq_made, 1)

            def leaders():
                dve.wait_ge(eq_made, 2 * ET)
                nc.vector.tensor_scalar(away[0:EP, :], dst_f[0:EP, :], -1.0, spare_f[0:EP, 0:1],
                                        ALU.mult, ALU.add).then_inc(lead_step, 1)
                dve.wait_ge(lead_step, 1)
                nc.vector.scalar_tensor_tensor(out=away[0:EP, :], in0=repeats[0:EP, :], scalar=0.0,
                                               in1=away[0:EP, :], op0=ALU.is_gt, op1=ALU.mult) \
                    .then_inc(lead_step, 1)
                dve.wait_ge(lead_step, 2)
                nc.vector.tensor_tensor(lead_i[0:EP, :], away[0:EP, :], dst_f[0:EP, :], ALU.add) \
                    .then_inc(lead_ready, 1)

            def slot(r, k, part):
                m = k - L_FINAL
                if live(r, m):
                    dve.wait_ge(O_ready, tile(r, m + 1))
                    if isinstance(r, int) and r * RING + m >= MAIN + ORING:
                        dve.wait_ge(scattered, 16 * (r * RING + m - MAIN - ORING + 1))
                    elif live(r, m - ORING):
                        dve.wait_ge(stored[m % ORING // 2], (r * (RING // ORING) + m // ORING) * 16)
                    nc.vector.tensor_tensor(outs[:, m % ORING, :], O[:, :], rows[:, m % RING, :], ALU.add) \
                        .then_inc(final_ready, 1)
                if live(r, k - L_HT):
                    dve.wait_ge(hT_hi_ready, tile(r, k - L_HT + 1))
                    if live(r, k - L_HT - 2):
                        dve.wait_ge(O_ready, tile(r, k - L_HT - 1))
                    nc.vector.tensor_tensor(hT_lo[k % 2][:, :], HT[:, 0:HID], hT_hi[k % 2][:, :].bitcast(F32),
                                            ALU.subtract).then_inc(hT_lo_ready, 1)
                if live(r, k + 1) and not without_vector(r, k, part):
                    dve.wait_ge(yT_hi_ready, tile(r, k + 2))
                    if live(r, k - 1):
                        dve.wait_ge(U_ready, tile(r, k))
                    nc.vector.tensor_tensor(yT_lo[(k + 1) % 2][:, :], yT[(k + 1) % 2][:, :],
                                            yT_hi[(k + 1) % 2][:, :].bitcast(F32), ALU.subtract) \
                        .then_inc(yT_lo_ready, 1)
                if isinstance(r, int) and r == 0 and k == 0:
                    dve.wait_ge(w_rounded, 2)
                    for h in range(HC):
                        last = nc.vector.tensor_tensor(w2_lo[:, h, :], w2_raw[h], w2_hi[:, h, :].bitcast(F32),
                                                       ALU.subtract)
                    last.then_inc(w_ready, 1)
                    dve.wait_ge(bias_hi_made, 1)
                    nc.vector.tensor_tensor(bias_rows[LO:LO + 1, :], C[LO:LO + 1, :], bias_hi.bitcast(F32),
                                            ALU.subtract) \
                        .then_inc(C_free, 1)
                a = k - L_SCALE
                c = a % 4
                if k % 2 == 0 and live(r, a):
                    dve.wait_ge(tanh_ready, r * PAIRS + k // 2)
                    nc.vector.scalar_tensor_tensor(out=scale[:, c:c + 2, 0], in0=th[:, c:c + 2], scalar=1.0,
                                                   in1=half_rstd[:, c:c + 2], op0=ALU.add, op1=ALU.mult)
                    nc.vector.scalar_tensor_tensor(out=scale[:, c:c + 2, 1], in0=th[:, c:c + 2], scalar=1.0,
                                                   in1=half_rstd[:, c:c + 2], op0=ALU.subtract, op1=ALU.mult,
                                                   reverse0=True).then_inc(scale_ready, 1)
                t, j = sum_tile(r, k, part)
                if t is not None:
                    dve.wait_ge(C_free, t + 1)
                    nc.vector.tensor_copy(same_now[0:EP, :], same[0:EP, bass.ds(t, 1), :]
                                          .rearrange("p a e -> p (a e)")).then_inc(same_ready, 1)
                def multiply_paths():
                    if part == "set0" and k == FIRST:
                        dve.wait_ge(attr_loaded, 32 * SETS)
                        dve.wait_ge(table_ready, 2)
                        dve.wait_ge(x1_ready, ET)
                    for j, path, number, (i1, i2) in load_segments(mybir.EngineType.DVE, r, k, part):
                        dve.wait_ge(prod_free, number + 1)
                        nc.vector.scalar_tensor_tensor(
                            out=prod[j % PB][0:EP, :, :], in0=x1[0:EP, set_tiles(part), bass.ds(i1, EXTENT)],
                            scalar=coef[0:EP, bass.ds(path, 1)], in1=x2[0:EP, set_tiles(part), bass.ds(i2, EXTENT)],
                            op0=ALU.mult, op1=ALU.mult).then_inc(multiplied, 1)
                if part in ("set0", "set1") and k % 2:
                    multiply_paths()
                if k % 2 and live(r, k):
                    dve.wait_ge(U_ready, tile(r, k + 1))
                if live(r, a):
                    dve.wait_ge(scale_ready, r * PAIRS + k // 2)
                    if live(r, a - 2):
                        dve.wait_ge(hsum_ready, tile(r, a - 1))
                    for i in range(2):
                        last = nc.vector.scalar_tensor_tensor(out=hid[k % 2][:, i, :], in0=U[a % 3][:, 0:HID],
                                                              scalar=scale[:, c, i:i + 1], in1=b1_bc[:, :],
                                                              op0=ALU.mult, op1=ALU.add)
                    last.then_inc(hid_in_ready, 1)
                if part in ("set0", "set1") and k % 2 == 0:
                    multiply_paths()
                if k % 2 and live(r, k):
                    pairs = r * PAIRS + (k + 1) // 2
                    c = (k - 1) % 4
                    nc.vector.max(top8[:, c, :], U[(k - 1) % 3][:, HID:WC])
                    nc.vector.max(top8[:, c + 1, :], U[k % 3][:, HID:WC]).then_inc(top_made, 1)
                    dve.wait_ge(top_made, pairs)
                    dve.wait_ge(rstd_ready, pairs)
                    for i in (c, c + 1):
                        last = nc.vector.scalar_tensor_tensor(out=half_gap[:, i:i + 1], in0=top8[:, i, 0:1],
                                                              scalar=top8[:, i, 1:2], in1=half_rstd[:, i:i + 1],
                                                              op0=ALU.subtract, op1=ALU.mult)
                    last.then_inc(half_gap_ready, 1)
                tiles = source_tiles(r, k - STATS_SLOT)
                if tiles:
                    dve.wait_ge(x1_loaded[tiles[0] // SET], 16 * SET)
                    dve.wait_ge(x1_loaded[tiles[-1] // SET], 16 * SET)
                    for t in tiles:
                        last = nc.vector.bn_stats(src_stats[0:EP, t, :], x1[0:EP, t, :])
                    last.then_inc(src_stats_made, 1)
                    dve.wait_ge(src_stats_made, k - STATS_SLOT + 1)
                    for t in tiles:
                        last = nc.vector.bn_aggr(src_mv[0:EP, t, :], src_stats[0:EP, t, :])
                    last.then_inc(src_var_ready, 1)
                tiles = source_tiles(r, k - STATS_SLOT - 2)
                if tiles:
                    tt = slice(tiles[0], tiles[-1] + 1)
                    dve.wait_ge(src_rstd_ready, k - STATS_SLOT - 1)
                    nc.vector.scalar_tensor_tensor(out=src_shift[0:EP, tt], in0=src_mv[0:EP, tt, 0],
                                                   scalar=-1.0, in1=src_rstd[0:EP, tt],
                                                   op0=ALU.mult, op1=ALU.mult).then_inc(src_shift_ready, 1)
                if isinstance(r, int) and r == 0 and k == FIRST - 1:
                    dve.wait_ge(table_loaded, 32)
                    by_path = table_raw.rearrange("o (n c) -> o n c", c=3)
                    nc.vector.tensor_copy(table[0:1, 0:2 * NP].rearrange("o (n c) -> o n c", c=2),
                                          by_path[:, :, 0:2]).then_inc(table_ready, 1)
                    nc.vector.tensor_copy(table[0:1, 2 * NP:3 * NP], by_path[:, :, 2]).then_inc(table_ready, 1)
                g = k - DST_SLOT
                if isinstance(r, int) and r == 0 and 0 <= g < ET // DST_GROUP:
                    for i in range(DST_GROUP):
                        repeats_of(DST_GROUP * g + i)
                    if g == ET // DST_GROUP - 1:
                        leaders()

            rounds(dve, slot)

        @block.gpsimd
        def _(pool):
            nc.gpsimd.memset(mean_mat, 1.0 / D).then_inc(pool_const, 1)
            nc.gpsimd.memset(twos, 2.0)
            nc.gpsimd.memset(ident[:, :], 0.0)
            nc.gpsimd.memset(later, 0.0).then_inc(pool_const, 1)
            pool.wait_ge(pool_const, 2)
            nc.gpsimd.affine_select(out=ident[:, :], in_=ident[:, :], compare_op=ALU.not_equal, fill=1.0,
                                    base=0, pattern=[[-1, P]], channel_multiplier=1).then_inc(pool_const, 1)
            nc.gpsimd.affine_select(out=later, in_=later, compare_op=ALU.is_ge, fill=1.0,
                                    base=0, pattern=[[-1, P]], channel_multiplier=1)
            nc.gpsimd.iota(spare_i[:, :], pattern=[[0, 1]], base=N, channel_multiplier=1).then_inc(pool_const, 1)
            nc.gpsimd.memset(minus_half[:, :], -0.5)
            nc.gpsimd.memset(ones[:, :].bitcast(F32), 1.0)
            nc.gpsimd.memset(bias_rows[:, :].bitcast(F32), 0.0).then_inc(bias_zero, 1)

            def fetch_sources(first, last):
                for t in range(first, last):
                    nc.gpsimd.indirect_dma_start(
                        out=x1[0:EP, t, :], out_offset=None, in_=x,
                        in_offset=bass.IndirectOffsetOnAxis(ap=src_i[0:EP, t:t + 1], axis=0),
                    ).then_inc(x1_loaded[t // SET], 16)

            pool.wait_ge(index_loaded, 32)
            fetch_sources(0, FETCH_FIRST)

            def slot(r, k, part):
                s = k - FIRST
                if isinstance(r, int) and r == 0 and s == 0:
                    pool.dma_start(y_rows[N:N + P, :], x[0:P, :]).then_inc(summed, 16)
                if isinstance(r, int) and r == 0 and k >= CLEAR_SLOT:
                    each = -(-ET // (FIRST + RING - CLEAR_SLOT))
                    if k == CLEAR_SLOT:
                        pool.wait_ge(eq_made, 2 * ET)
                    for i in range(each * (k - CLEAR_SLOT), min(ET, each * (k - CLEAR_SLOT + 1))):
                        last = nc.gpsimd.memset(acc[0:EP, (dst_tiles + i) % ET, :], 0.0)
                        if i == ET - 1:
                            last.then_inc(prod_free, PB)

                adds = []
                if part in ("set0", "set1") and k > FIRST:
                    if part == "set0" and k == FIRST + 1:
                        pool.wait_ge(table_ready, 2)
                    adds = load_segments(mybir.EngineType.Pool, r, k - 1, part)

                def add_product(j, path, number, segment):
                    pool.wait_ge(multiplied, number + 1)
                    pool.wait_ge(prod_free, number + PB)
                    sums = acc[0:EP, set_tiles(part), bass.ds(segment[0], EXTENT)]
                    nc.gpsimd.tensor_tensor(sums, sums, prod[j % PB][0:EP, :, :], ALU.add).then_inc(prod_free, 1)

                for item in adds[:1]:
                    add_product(*item)
                t0, j0 = sum_tile(r, k - 2, part) if s >= 2 else (None, None)
                if t0 is not None:
                    pool.wait_ge(summed, t0 * 16 + 16)
                    pool.wait_ge(C_free, t0 + 2)
                if part == "set1" and s == 0:
                    pool.wait_ge(y_filled, 16 * FILLS)
                    pool.wait_ge(summed, (r - SET1[0]) * (SET // 2) * 16 + 16)
                if part == "set1" and s == 1:
                    pool.wait_ge(index_copied, r - SET1[0] + 1)
                if k % 2 and live(r, k):
                    pool.wait_ge(squares_ready, tile(r, k + 1))
                    if live(r, k - 4):
                        pool.wait_ge(scale_ready, r * PAIRS + k // 2 - 1)
                a = k - L_SUM
                if live(r, a):
                    pool.wait_ge(hid_ready, tile(r, a + 1))
                    if live(r, a - 2):
                        pool.wait_ge(HT_ready, tile(r, a - 1))
                    nc.gpsimd.tensor_tensor(hsum[a % 2][:, :], hid[a % 2][:, 0, :], hid[a % 2][:, 1, :], ALU.add) \
                        .then_inc(hsum_ready, 1)
                for item in adds[1:2]:
                    add_product(*item)
                if part == "set1" and s == 0:
                    pool.wait_ge(lead_ready, 1)
                    t = (r - SET1[0]) * (SET // 2)
                    nc.gpsimd.tensor_copy(put_i[0:EP, :], lead_i[0:EP, bass.ds(t, SET // 2)]) \
                        .then_inc(index_copied, 1)
                if k % 2 and live(r, k):
                    c = (k - 1) % 4
                    nc.gpsimd.tensor_scalar(var4[:, c:c + 2], squares[:, c:c + 2], 4.0 / D, 4.0 * EPS,
                                            ALU.mult, ALU.add).then_inc(var4_made, 1)
                    pool.wait_ge(var4_made, r * PAIRS + k // 2 + 1)
                    nc.gpsimd.tensor_tensor(half_rstd[:, c:c + 2], var4[:, c:c + 2], minus_half[:, 0:2],
                                            ALU.pow).then_inc(rstd_ready, 1)

                for item in adds[2:]:
                    add_product(*item)

                if isinstance(r, int) and r == 0 and 0 <= k and FETCH_FIRST + FETCH * k < ET:
                    fetch_sources(FETCH_FIRST + FETCH * k, min(ET, FETCH_FIRST + FETCH * (k + 1)))
                tiles = source_tiles(r, k - NORM_SLOT)
                for t in tiles[2:]:
                    pool.wait_ge(src_shift_ready, k - NORM_SLOT + 1)
                    nc.gpsimd.tensor_scalar(x1[0:EP, t, :], x1[0:EP, t, :], src_rstd[0:EP, t:t + 1],
                                            src_shift[0:EP, t:t + 1], ALU.mult, ALU.add).then_inc(x1_ready, 1)
                tiles = source_tiles(r, k - STATS_SLOT - 1)
                if tiles:
                    tt = slice(tiles[0], tiles[-1] + 1)
                    pool.wait_ge(src_var_ready, k - STATS_SLOT)
                    nc.gpsimd.tensor_scalar(src_rstd[0:EP, tt], src_mv[0:EP, tt, 1], EPS, 1.0,
                                            ALU.add, ALU.mult).then_inc(src_rstd_step, 1)
                    pool.wait_ge(src_rstd_step, k - STATS_SLOT)
                    nc.gpsimd.tensor_tensor(src_rstd[0:EP, tt], src_rstd[0:EP, tt], minus_half[0:EP, 0:len(tiles)],
                                            ALU.pow).then_inc(src_rstd_ready, 1)
                if t0 is not None:
                    where = put_i[0:EP, s // 2 - 1:s // 2] if part == "set1" else lead_i[0:EP, t0:t0 + 1]
                    nc.gpsimd.indirect_dma_start(
                        out=y_rows, out_offset=bass.IndirectOffsetOnAxis(ap=where, axis=0),
                        in_=moved[j0][0:EP, :], in_offset=None, compute_op=ALU.add).then_inc(summed, 16)
                if isinstance(r, int) and MAIN <= r * RING + k + L_GATHER < TILES:
                    m = r * RING + k + L_GATHER
                    if m == MAIN:
                        pool.wait_ge(summed, 16 * ET + 16)
                    pool.wait_ge(final_ready, m - RING + 1)
                    nc.gpsimd.indirect_dma_start(
                        out=rows[0:EP, m % RING, :], out_offset=None, in_=y_rows,
                        in_offset=bass.IndirectOffsetOnAxis(ap=dst_i[0:EP, m - MAIN:m - MAIN + 1], axis=0),
                    ).then_inc(edge_loaded[m % RING], 16)
                if isinstance(r, int) and MAIN <= r * RING + k - L_STORE < TILES:
                    m = r * RING + k - L_STORE
                    if m == MAIN:
                        for i in range(2):
                            pool.wait_ge(stored[i], 16 * (MAIN_PAIRS // 2))
                    pool.wait_ge(final_ready, m + 1)
                    if m > MAIN:
                        pool.wait_ge(scattered, 16 * (m - MAIN))
                    nc.gpsimd.indirect_dma_start(
                        out=out, out_offset=bass.IndirectOffsetOnAxis(ap=lead_i[0:EP, m - MAIN:m - MAIN + 1], axis=0),
                        in_=outs[0:EP, m % ORING, :], in_offset=None,
                        bounds_check=N - 1, oob_is_err=False).then_inc(scattered, 16)

            rounds(pool, slot)
            pool.wait_ge(scattered, 16 * ET)

        @block.tensor
        def _(pe):
            pe.wait_ge(pool_const, 4)
            pe.wait_ge(w_loaded, 16 * (DC + 1))
            for c in range(DC):
                last = nc.tensor.matmul(U[0][:, 0:WC], mean_mat, w_raw[:, c, :], start=(c == 0), stop=(c == DC - 1))
            last.then_inc(col_mean, 1)
            pe.wait_ge(bias_loaded, 32)
            nc.tensor.matmul(C[:, :], twos[0:EXPERTS, :], b2_raw, start=True, stop=True).then_inc(bias_sum, 1)

            def slot(r, k, part):
                m = k - L_HT
                if live(r, m):
                    pe.wait_ge(hsum_ready, tile(r, m + 1))
                    if live(r, m - 1):
                        pe.wait_ge(hT_lo_ready, tile(r, m))
                    for h in range(HC):
                        last = nc.tensor.transpose(HT[:, h * P:(h + 1) * P], hsum[m % 2][:, h * P:(h + 1) * P],
                                                   ident[:, :])
                    last.then_inc(HT_ready, 1)
                if live(r, k + 1):
                    wait_rows(pe, r, k + 1)
                    if live(r, k - 1):
                        pe.wait_ge(yT_lo_ready, tile(r, k))
                    for c in range(DC):
                        last = nc.tensor.matmul(yT[(k + 1) % 2][:, c * P:(c + 1) * P],
                                                rows[:, (k + 1) % RING, c * P:(c + 1) * P], ident[:, :],
                                                is_transpose=True, start=(c == 0), stop=(c == DC - 1),
                                                skip_group_check=True)
                    last.then_inc(yT_ready, 1)
                if live(r, k):
                    if isinstance(r, int) and r == 0 and k == 0:
                        pe.wait_ge(w_ready, 1)
                    pe.wait_ge(yT_lo_ready, tile(r, k + 1))
                    if live(r, k - 3):
                        pe.wait_ge(hid_in_ready, tile(r, k - 2))
                    u = U[k % 3][:, 0:WC]
                    hi, lo = yT_hi[k % 2], yT_lo[k % 2]
                    for c in range(DC):
                        cc = slice(c * P, (c + 1) * P)
                        nc.tensor.matmul(u, hi[:, cc], w_hi[:, c, :], start=(c == 0), stop=False)
                        nc.tensor.matmul(u, hi[:, cc], w_lo[:, c, :], start=False, stop=False)
                        last = nc.tensor.matmul(u, lo[:, cc], w_hi[:, c, :], start=False, stop=(c == DC - 1))
                    last.then_inc(U_ready, 1)
                if live(r, k + 1) and without_vector(r, k, part):
                    pe.wait_ge(yT_hi_ready, tile(r, k + 2))
                    nc.tensor.matmul(yT[(k + 1) % 2][:, :], minus_ident[:, :], yT_hi[(k + 1) % 2][:, :],
                                     start=False, stop=True, skip_group_check=True).then_inc(yT_less_ready, 1)
                m = k - L_DOWN
                if live(r, m):
                    if isinstance(r, int) and r * RING + m == 0:
                        pe.wait_ge(C_free, 1)
                        pe.wait_ge(w_ready, 2)
                    if live(r, m - 1):
                        pe.wait_ge(final_ready, tile(r, m))
                    nc.tensor.matmul(O[:, :], ones[:, :], bias_rows[:, :], start=True, stop=False)
                    pe.wait_ge(hT_lo_ready, tile(r, m + 1))
                    hi, lo = hT_hi[m % 2], hT_lo[m % 2]
                    for h in range(HC):
                        hh = slice(h * P, (h + 1) * P)
                        nc.tensor.matmul(O[:, :], hi[:, hh], w2_hi[:, h, :], start=False, stop=False)
                        nc.tensor.matmul(O[:, :], hi[:, hh], w2_lo[:, h, :], start=False, stop=False)
                        last = nc.tensor.matmul(O[:, :], lo[:, hh], w2_hi[:, h, :], start=False, stop=(h == HC - 1))
                    last.then_inc(O_ready, 1)
                t, j = sum_tile(r, k, part)
                if t is not None:
                    if k == FIRST:
                        pe.wait_ge(prod_free, PB + (NP if part == "set1" else 2 * NP))
                    pe.wait_ge(same_ready, t + 1)
                    pe.wait_ge(C_free, t + 1)
                    nc.tensor.matmul(C[0:EP, :], same_now[0:EP, :],
                                     acc[0:EP, bass.ds(t, 1), :].rearrange("p a d -> p (a d)"),
                                     start=True, stop=True).then_inc(comb_ready, 1)

            rounds(pe, slot)


_INS = ["x", "src", "dst", "edge_attr_512", "L0_gnn_path_coeffs", "L0_gnn_path_indices",
        "L0_ffn_Wg", "L0_ffn_W1", "L0_ffn_b1", "L0_ffn_W2", "L0_ffn_b2"]


def kernel(**inputs):
    import numpy as _np
    import concourse.bacc as _bacc
    from concourse import mybir as _mybir
    from concourse.bass_utils import run_bass_kernel_spmd as _run

    nc = _bacc.Bacc("TRN2", target_bir_lowering=False, num_devices=1)
    arrays, args = {}, []
    for name in _INS:
        a = _np.ascontiguousarray(inputs[name])
        arrays[f"in_{name}"] = a
        args.append(nc.dram_tensor(f"in_{name}", a.shape, _mybir.dt.from_np(a.dtype), kind="ExternalInput").ap())
    shape = inputs["x"].shape
    args.append(nc.dram_tensor("out_rows", shape, _mybir.dt.float32, kind="ExternalOutput").ap())
    gnn_ffn_kernel(nc, *args)
    r = _run(nc, [arrays], core_ids=[0])
    return r.results[0]["out_rows"]
```
